# Optimizing a Trainium2 kernel written in Bass

```python
import numpy as np
import jax
import jax.numpy as jnp

def _softmax(x, axis=-1):
    return jax.nn.softmax(x, axis=axis)

def _gelu(x):
    return jax.nn.gelu(x, approximate=True)

def _silu(x):
    return jax.nn.silu(x)

def _sigmoid(x):
    return jax.nn.sigmoid(x)

def _layernorm(x, axis=-1, eps=1e-05):
    m = jnp.mean(x, axis=axis, keepdims=True)
    v = jnp.var(x, axis=axis, keepdims=True)
    return (x - m) / jnp.sqrt(v + eps)

def _scatter_add(tgt, idx, src, axis=0):
    return tgt.at[idx].add(src)

def _segment_sum(src, seg, n):
    return jax.ops.segment_sum(src, seg, n)
kernel_name = 'mk_gnn_preln_d4_gnn_r32_c3ee73'

def setup_inputs(seed: int=0):
    np.random.seed(seed)
    _w = jnp.asarray

    def _rec_inputs():
        import jax
        import jax.numpy as jnp
        _gk = jax.random.key(seed)
        x = -0.0003713 + 1 * jax.random.normal(jax.random.fold_in(_gk, 1), (3125, 128), jnp.float32)
        src = jax.random.randint(jax.random.fold_in(_gk, 2), (100000,), 0, 3125, jnp.int32)
        dst = jnp.minimum((3125 * jax.random.uniform(jax.random.fold_in(_gk, 3), (100000,)) ** 2.0).astype(jnp.int32), 99999)
        _o = jnp.argsort(dst, stable=True)
        src = src[_o]
        dst = dst[_o]
        edge_type_32 = jax.random.randint(jax.random.fold_in(_gk, 13), (100000,), 0, 32, jnp.int32)
        edge_weight = jax.random.uniform(jax.random.fold_in(_gk, 14), (100000,), jnp.float32, 0.0, 1)
        edge_weight1 = jax.random.uniform(jax.random.fold_in(_gk, 15), (100000, 1), jnp.float32, 0.0, 0.999998)
        return (x, src, dst, edge_type_32, edge_weight, edge_weight1)
    x, src, dst, edge_type_32, edge_weight, edge_weight1 = _rec_inputs()

    def _L0_gnn_setup():
        import jax, jax.numpy as jnp
        import numpy as np
        N = 3125
        E = 18750
        F_IN = 128
        F_OUT = 128

        def _l2norm(v):
            return v / (jnp.linalg.norm(v) + 1e-12)
        key = jax.random.key(seed)
        k1, k2, k3, k4 = jax.random.split(key, 4)
        x = jax.random.normal(k1, (N, F_IN), dtype=jnp.float32)
        edge_index = jax.random.randint(k2, (2, E), 0, N, dtype=jnp.int32)
        edge_wt = jnp.ones((E,), dtype=jnp.float32)
        weight = jax.random.normal(k3, (F_IN, F_OUT), dtype=jnp.float32) / np.sqrt(F_IN).astype(np.float32)
        bias = jnp.zeros((F_OUT,), dtype=jnp.float32)
        u = jax.random.normal(k4, (F_IN,), dtype=jnp.float32)
        return {'x': x, 'edge_index': edge_index, 'edge_wt': edge_wt, 'weight': weight, 'bias': bias, 'u': u}
    _L0_gnn_all = _L0_gnn_setup()
    _L0_gnn_in = {k: v for k, v in _L0_gnn_all.items() if k in ('weight', 'bias', 'u')}
    del _L0_gnn_all

    def _L1_gnn_setup():
        import jax, jax.numpy as jnp
        import numpy as np
        N, E, D, F, R, B = (50000, 50000, 128, 128, 32, 8)
        key = jax.random.key(seed)
        ks = jax.random.split(key, 9)
        h = jax.random.normal(ks[0], (N, D), dtype=jnp.float32)
        src = jax.random.randint(ks[1], (E,), 0, N, dtype=jnp.int32)
        dst = jax.random.randint(ks[2], (E,), 0, N, dtype=jnp.int32)
        etype = jax.random.randint(ks[3], (E,), 0, R, dtype=jnp.int32)
        norm = jax.random.uniform(ks[4], (E, 1), dtype=jnp.float32)
        weight = jax.random.normal(ks[5], (B, D, F), dtype=jnp.float32) * (2.0 / (D + F)) ** 0.5
        w_comp = jax.random.normal(ks[6], (R, B), dtype=jnp.float32) * (2.0 / (R + B)) ** 0.5
        loop_weight = jax.random.normal(ks[7], (D, F), dtype=jnp.float32) * (2.0 / (D + F)) ** 0.5
        h_bias = jnp.zeros((F,), dtype=jnp.float32)
        return {'h': h, 'src': src, 'dst': dst, 'etype': etype, 'norm': norm, 'weight': weight, 'w_comp': w_comp, 'loop_weight': loop_weight, 'h_bias': h_bias}
    _L1_gnn_all = _L1_gnn_setup()
    _L1_gnn_in = {k: v for k, v in _L1_gnn_all.items() if k in ('weight', 'w_comp', 'loop_weight', 'h_bias')}
    del _L1_gnn_all

    def _L2_gnn_setup():
        import jax, jax.numpy as jnp
        import numpy as np
        N_NODES = 3125
        N_EDGES = 100000
        D_IN = 128
        D_OUT = 128
        key = jax.random.key(seed)
        k1, k2, k3, k4, k5, k6 = jax.random.split(key, 6)
        x = jax.random.normal(k1, (N_NODES, D_IN), dtype=jnp.float32)
        W = jax.random.normal(k2, (D_OUT, D_IN), dtype=jnp.float32) * (1.0 / np.sqrt(D_IN))
        bias = jnp.zeros((D_OUT,), dtype=jnp.float32)
        prelu_a = jnp.full((1,), 0.25, dtype=jnp.float32)
        edge_val = jax.random.uniform(k3, (N_EDGES,), dtype=jnp.float32)
        edge_src = jax.random.randint(k4, (N_EDGES,), 0, N_NODES, dtype=jnp.int32)
        edge_dst = jax.random.randint(k5, (N_EDGES,), 0, N_NODES, dtype=jnp.int32)
        return {'x': x, 'W': W, 'bias': bias, 'prelu_a': prelu_a, 'edge_val': edge_val, 'edge_src': edge_src, 'edge_dst': edge_dst}
    _L2_gnn_all = _L2_gnn_setup()
    _L2_gnn_in = {k: v for k, v in _L2_gnn_all.items() if k in ('W', 'bias', 'prelu_a')}
    del _L2_gnn_all

    def _L3_gnn_setup():
        import jax, jax.numpy as jnp
        import numpy as np
        N = 50000
        IN_DIM = 128
        OUT_DIM = 128
        HEADS = 2
        EPS = 1e-05
        NEG_SLOPE = 0.2

        def _add_self_loops(edge_index, num_nodes):
            loop = jnp.arange(num_nodes, dtype=edge_index.dtype)
            src = jnp.concatenate([edge_index[0], loop])
            dst = jnp.concatenate([edge_index[1], loop])
            return (src, dst)

        def _layernorm(h, gamma, beta):
            mu = jnp.mean(h, axis=-1, keepdims=True)
            var = jnp.mean(jnp.square(h - mu), axis=-1, keepdims=True)
            return (h - mu) * jax.lax.rsqrt(var + EPS) * gamma + beta

        def _silu(h):
            return h * jax.nn.sigmoid(h)

        def _gcn_conv(x, src, dst, W, b, num_nodes):
            h = x @ W
            deg = jnp.zeros((num_nodes,), h.dtype).at[dst].add(1.0)
            dinv = jnp.where(deg > 0, jax.lax.rsqrt(jnp.maximum(deg, 1.0)), 0.0)
            norm = dinv[src] * dinv[dst]
            msg = h[src] * norm[:, None]
            out = jnp.zeros((num_nodes, h.shape[1]), h.dtype).at[dst].add(msg)
            return out + b

        def _gat_conv(x, src, dst, W, att_src, att_dst, b, num_nodes, heads):
            C = W.shape[1] // heads
            h = (x @ W).reshape(num_nodes, heads, C)
            a_src = jnp.sum(h * att_src, axis=-1)
            a_dst = jnp.sum(h * att_dst, axis=-1)
            e = a_src[src] + a_dst[dst]
            e = jnp.where(e > 0, e, NEG_SLOPE * e)
            m = jax.ops.segment_max(e, dst, num_segments=num_nodes)
            ex = jnp.exp(e - m[dst])
            den = jax.ops.segment_sum(ex, dst, num_segments=num_nodes)
            alpha = ex / den[dst]
            msg = h[src] * alpha[:, :, None]
            out = jnp.zeros((num_nodes, heads, C), h.dtype).at[dst].add(msg)
            return jnp.mean(out, axis=1) + b
        key = jax.random.key(seed)
        ks = jax.random.split(key, 9)
        x = jax.random.normal(ks[0], (N, IN_DIM), dtype=jnp.float32)
        edge_index = jax.random.randint(ks[1], (2, 25000), 0, N, dtype=jnp.int64)
        s = 1.0 / np.sqrt(IN_DIM)
        gcn_w = jax.random.uniform(ks[2], (IN_DIM, OUT_DIM), jnp.float32, -s, s)
        gcn_b = jnp.zeros((OUT_DIM,), jnp.float32)
        so = 1.0 / np.sqrt(OUT_DIM)
        gat_w = jax.random.uniform(ks[3], (OUT_DIM, HEADS * OUT_DIM), jnp.float32, -so, so)
        att_src = jax.random.uniform(ks[4], (HEADS, OUT_DIM), jnp.float32, -so, so)
        att_dst = jax.random.uniform(ks[5], (HEADS, OUT_DIM), jnp.float32, -so, so)
        gat_b = jnp.zeros((OUT_DIM,), jnp.float32)
        ln_gamma = jnp.ones((OUT_DIM,), jnp.float32)
        ln_beta = jnp.zeros((OUT_DIM,), jnp.float32)
        return dict(x=x, edge_index=edge_index, gcn_w=gcn_w, gcn_b=gcn_b, gat_w=gat_w, att_src=att_src, att_dst=att_dst, gat_b=gat_b, ln_gamma=ln_gamma, ln_beta=ln_beta)
    _L3_gnn_all = _L3_gnn_setup()
    _L3_gnn_in = {k: v for k, v in _L3_gnn_all.items() if k in ('gcn_w', 'gcn_b', 'gat_w', 'att_src', 'att_dst', 'gat_b', 'ln_gamma', 'ln_beta')}
    del _L3_gnn_all
    return {'x': x, 'src': src, 'dst': dst, 'edge_type_32': edge_type_32, 'edge_weight': edge_weight, 'edge_weight1': edge_weight1, 'L0_gnn_weight': _L0_gnn_in['weight'], 'L0_gnn_bias': _L0_gnn_in['bias'], 'L0_gnn_u': _L0_gnn_in['u'], 'L1_gnn_weight': _L1_gnn_in['weight'], 'L1_gnn_w_comp': _L1_gnn_in['w_comp'], 'L1_gnn_loop_weight': _L1_gnn_in['loop_weight'], 'L1_gnn_h_bias': _L1_gnn_in['h_bias'], 'L2_gnn_W': _L2_gnn_in['W'], 'L2_gnn_bias': _L2_gnn_in['bias'], 'L2_gnn_prelu_a': _L2_gnn_in['prelu_a'], 'L3_gnn_gcn_w': _L3_gnn_in['gcn_w'], 'L3_gnn_gcn_b': _L3_gnn_in['gcn_b'], 'L3_gnn_gat_w': _L3_gnn_in['gat_w'], 'L3_gnn_att_src': _L3_gnn_in['att_src'], 'L3_gnn_att_dst': _L3_gnn_in['att_dst'], 'L3_gnn_gat_b': _L3_gnn_in['gat_b'], 'L3_gnn_ln_gamma': _L3_gnn_in['ln_gamma'], 'L3_gnn_ln_beta': _L3_gnn_in['ln_beta']}

def reference(x, src, dst, edge_type_32, edge_weight, edge_weight1, L0_gnn_weight, L0_gnn_bias, L0_gnn_u, L1_gnn_weight, L1_gnn_w_comp, L1_gnn_loop_weight, L1_gnn_h_bias, L2_gnn_W, L2_gnn_bias, L2_gnn_prelu_a, L3_gnn_gcn_w, L3_gnn_gcn_b, L3_gnn_gat_w, L3_gnn_att_src, L3_gnn_att_dst, L3_gnn_gat_b, L3_gnn_ln_gamma, L3_gnn_ln_beta):
    import jax
    import jax.numpy as jnp

    def _L0_gnn_ref(x, edge_index, edge_wt, weight, bias, u):
        import jax, jax.numpy as jnp
        import numpy as np
        N = 3125
        E = 18750
        F_IN = 128
        F_OUT = 128

        def _l2norm(v):
            return v / (jnp.linalg.norm(v) + 1e-12)
        W_sg = jax.lax.stop_gradient(weight)
        v = _l2norm(W_sg.T @ jax.lax.stop_gradient(u))
        u1 = _l2norm(W_sg @ v)
        sigma = u1 @ (weight @ v)
        W_sn = weight / sigma
        w = jax.nn.sigmoid(edge_wt)
        row, col = (edge_index[0], edge_index[1])
        loop = jnp.arange(N, dtype=edge_index.dtype)
        row_a = jnp.concatenate([row, loop])
        col_a = jnp.concatenate([col, loop])
        w_a = jnp.concatenate([w, jnp.ones((N,), w.dtype)])
        deg = jax.ops.segment_sum(w_a, col_a, num_segments=N)
        dinv = jnp.where(deg > 0, deg ** (-0.5), 0.0)
        norm = dinv[row_a] * w_a * dinv[col_a]
        xw = x @ W_sn
        msgs = norm[:, None] * xw[row_a]
        out = jax.ops.segment_sum(msgs, col_a, num_segments=N) + bias
        return out

    def _L1_gnn_ref(h, src, dst, etype, norm, weight, w_comp, loop_weight, h_bias):
        import jax, jax.numpy as jnp
        import numpy as np
        N, E, D, F, R, B = (50000, 50000, 128, 128, 32, 8)
        n_nodes, d_in = h.shape
        n_rels = w_comp.shape[0]
        W_rel = jnp.einsum('rb,bdf->rdf', w_comp, weight)
        seg = etype * n_nodes + dst
        agg = jax.ops.segment_sum(h[src] * norm, seg, num_segments=n_rels * n_nodes)
        agg = agg.reshape(n_rels, n_nodes, d_in)
        node_repr = jnp.einsum('rnd,rdf->nf', agg, W_rel)
        node_repr = node_repr + h_bias + h @ loop_weight
        return jax.nn.relu(node_repr)

    def _L2_gnn_ref(x, W, bias, prelu_a, edge_val, edge_src, edge_dst):
        import jax, jax.numpy as jnp
        import numpy as np
        N_NODES = 3125
        N_EDGES = 100000
        D_IN = 128
        D_OUT = 128
        h = jnp.einsum('ni,oi->no', x, W)
        msgs = edge_val[:, None] * h[edge_dst]
        out = jax.ops.segment_sum(msgs, edge_src, num_segments=N_NODES)
        out = out + bias
        out = jnp.where(out >= 0, out, prelu_a[0] * out)
        return out

    def _L3_gnn_ref(x, edge_index, gcn_w, gcn_b, gat_w, att_src, att_dst, gat_b, ln_gamma, ln_beta):
        import jax, jax.numpy as jnp
        import numpy as np
        N = 50000
        IN_DIM = 128
        OUT_DIM = 128
        HEADS = 2
        EPS = 1e-05
        NEG_SLOPE = 0.2

        def _add_self_loops(edge_index, num_nodes):
            loop = jnp.arange(num_nodes, dtype=edge_index.dtype)
            src = jnp.concatenate([edge_index[0], loop])
            dst = jnp.concatenate([edge_index[1], loop])
            return (src, dst)

        def _layernorm(h, gamma, beta):
            mu = jnp.mean(h, axis=-1, keepdims=True)
            var = jnp.mean(jnp.square(h - mu), axis=-1, keepdims=True)
            return (h - mu) * jax.lax.rsqrt(var + EPS) * gamma + beta

        def _silu(h):
            return h * jax.nn.sigmoid(h)

        def _gcn_conv(x, src, dst, W, b, num_nodes):
            h = x @ W
            deg = jnp.zeros((num_nodes,), h.dtype).at[dst].add(1.0)
            dinv = jnp.where(deg > 0, jax.lax.rsqrt(jnp.maximum(deg, 1.0)), 0.0)
            norm = dinv[src] * dinv[dst]
            msg = h[src] * norm[:, None]
            out = jnp.zeros((num_nodes, h.shape[1]), h.dtype).at[dst].add(msg)
            return out + b

        def _gat_conv(x, src, dst, W, att_src, att_dst, b, num_nodes, heads):
            C = W.shape[1] // heads
            h = (x @ W).reshape(num_nodes, heads, C)
            a_src = jnp.sum(h * att_src, axis=-1)
            a_dst = jnp.sum(h * att_dst, axis=-1)
            e = a_src[src] + a_dst[dst]
            e = jnp.where(e > 0, e, NEG_SLOPE * e)
            m = jax.ops.segment_max(e, dst, num_segments=num_nodes)
            ex = jnp.exp(e - m[dst])
            den = jax.ops.segment_sum(ex, dst, num_segments=num_nodes)
            alpha = ex / den[dst]
            msg = h[src] * alpha[:, :, None]
            out = jnp.zeros((num_nodes, heads, C), h.dtype).at[dst].add(msg)
            return jnp.mean(out, axis=1) + b
        num_nodes = x.shape[0]
        src, dst = _add_self_loops(edge_index, num_nodes)
        h = _gcn_conv(x, src, dst, gcn_w, gcn_b, num_nodes)
        h = _silu(_layernorm(h, ln_gamma, ln_beta))
        h = _gat_conv(h, src, dst, gat_w, att_src, att_dst, gat_b, num_nodes, HEADS)
        h = _silu(_layernorm(h, ln_gamma, ln_beta))
        return h
    edge_index = jnp.stack([src, dst])
    h = jnp.maximum(_layernorm(x, axis=-1), 0.0)
    x = x + _L0_gnn_ref(h, edge_index, edge_weight, L0_gnn_weight, L0_gnn_bias, L0_gnn_u)
    h = jnp.maximum(_layernorm(x, axis=-1), 0.0)
    x = x + _L1_gnn_ref(h, src, dst, edge_type_32, edge_weight1, L1_gnn_weight, L1_gnn_w_comp, L1_gnn_loop_weight, L1_gnn_h_bias)
    h = jnp.maximum(_layernorm(x, axis=-1), 0.0)
    x = x + _L2_gnn_ref(h, L2_gnn_W, L2_gnn_bias, L2_gnn_prelu_a, edge_weight, src, dst)
    h = jnp.maximum(_layernorm(x, axis=-1), 0.0)
    x = x + _L3_gnn_ref(h, edge_index, L3_gnn_gcn_w, L3_gnn_gcn_b, L3_gnn_gat_w, L3_gnn_att_src, L3_gnn_att_dst, L3_gnn_gat_b, L3_gnn_ln_gamma, L3_gnn_ln_beta)
    return x

_drawn_inputs = setup_inputs


def setup_inputs(seed=0):
    import zlib

    import numpy as np

    out = dict(_drawn_inputs(seed))
    spreads = {'L0_gnn_bias': (0.0, 0.1),
     'L1_gnn_h_bias': (0.0, 0.1),
     'L2_gnn_bias': (0.0, 0.707),
     'L3_gnn_gcn_b': (0.0, 0.307),
     'L3_gnn_gat_b': (0.0, 0.1),
     'L3_gnn_ln_gamma': (1.0, 0.542),
     'L3_gnn_ln_beta': (0.0, 0.703)}
    factors = {'L0_gnn_u': 28.893, 'L3_gnn_att_src': 64.0, 'L3_gnn_att_dst': 64.0}
    for name, (base, spread) in spreads.items():
        noise = np.random.default_rng([zlib.crc32(name.encode()), seed]).standard_normal(out[name].shape)
        drawn = base * np.exp(spread * noise) if base else spread * noise
        out[name] = jnp.asarray(drawn.astype(out[name].dtype))
    for name, factor in factors.items():
        out[name] = (out[name] * factor).astype(out[name].dtype)
    return out
```

```python
import concourse.bass as bass
from concourse import mybir
from contextlib import ExitStack

F32 = mybir.dt.float32
BF16 = mybir.dt.bfloat16
F16 = mybir.dt.float16
I32 = mybir.dt.int32
ALU = mybir.AluOpType
ACT = mybir.ActivationFunctionType
AX = mybir.AxisListType

P = 128
N = 3125
F = 128
E = 100000
R = 32
B = 8
NT = -(-N // P)
TAIL = N - (NT - 1) * P
W = 2 * P
NW = -(-N // W)
CELLS = NT * NW
CW = CELLS + (-CELLS) % 8
EP = 125
EC = E // EP
G = 8
KS = 4
T = -(-((E + CELLS * P) // P) // (4 * G)) * 4 * G
NR = 8
(S_LOC, D_LOC, W_SIG, W_RAW, W_REL, SRC, SRC_REL, DST, CELL, D_LO, D_HI, W_A, W_B, W_C, NF) = range(15)
SAME = DST
EPS = 1e-05


VECS = ["L0_gnn_bias", "L1_gnn_h_bias", "L2_gnn_bias", "L3_gnn_gcn_b", "L3_gnn_gat_b", "L3_gnn_ln_gamma", "L3_gnn_ln_beta"]
(B0, B1, B2, B_GCN, B_GAT, GAMMA, BETA) = range(len(VECS))
NTAB = -(-T // P)


def linker(eng, sem, base=0):
    count = [0]

    def link(ins):
        count[0] += 1
        ins.then_inc(sem, 1)
        eng.wait_ge(sem, base + count[0])
        return count[0]
    return link


def bcast(ap, shape):
    return ap.broadcast_to(shape)


def layer_norm(nc, v, link, var_ready, std_ready, out, x, scratch, sq, st, relu=True, nth=1):
    full = [P, NT, F]
    mean, rstd = st[:, 0, :], st[:, 1, :]
    link(nc.vector.tensor_reduce(mean, x, AX.X, ALU.add))
    link(nc.vector.tensor_scalar(mean, mean, 1.0 / F, None, ALU.mult))
    link(nc.vector.tensor_tensor(scratch, x, bcast(mean.unsqueeze(2), full), ALU.subtract))
    link(nc.vector.tensor_tensor(sq, scratch, scratch, ALU.mult))
    link(nc.vector.tensor_reduce(rstd, sq, AX.X, ALU.add))
    nc.vector.tensor_scalar(rstd, rstd, 1.0 / F, EPS, ALU.mult, ALU.add).then_inc(var_ready, 1)
    v.wait_ge(std_ready, nth)
    link(nc.vector.reciprocal(rstd, rstd))
    link(nc.vector.tensor_tensor(out, scratch, bcast(rstd.unsqueeze(2), full), ALU.mult))
    if relu:
        link(nc.vector.tensor_scalar(out, out, 0.0, None, ALU.max))


def root_of_variance(nc, act, var_ready, std_ready, st, nth=1):
    act.wait_ge(var_ready, nth)
    nc.scalar.activation(st[:, 1, :], st[:, 1, :], ACT.Sqrt).then_inc(std_ready, 1)


def program(nc, A, out):
    with ExitStack() as ctx:
        ctx.enter_context(nc.allow_non_contiguous_dma(reason="small tables"))
        sb = lambda name, shape, dt, c=ctx: c.enter_context(nc.sbuf_tensor(name, shape, dt))
        ps = lambda name, shape, dt, c=ctx: c.enter_context(nc.psum_tensor(name, shape, dt))
        sem = lambda name: ctx.enter_context(nc.semaphore(name))
        dram = lambda name, shape, dt: nc.dram_tensor(name, shape, dt).ap()

        M = {}
        M["x"] = sb("x", [P, NT, F], F32)
        M["h"] = sb("h", [P, NT, F], F32)
        M["ident"] = sb("ident", [P, P], F32)
        M["identb"] = sb("identb", [P, P], BF16)
        M["iota_w"] = sb("iota_w", [P, W], BF16)
        M["iota_f"] = sb("iota_f", [P, W], F32)
        M["zeros"] = sb("zeros", [P, 512], BF16)
        M["ones"] = sb("ones", [P, P], F32)
        M["deg"] = sb("deg", [P, 4, NT], F32)
        M["wrel"] = sb("wrel", [P, R, F], F32)
        M["stats"] = sb("stats", [P, 2, NT], F32)
        M["start_row"] = sb("start_row", [P, CELLS], F32)
        M["hT"] = sb("hT", [P, NT, P], F32)
        M["vec"] = sb("vec", [P, len(VECS), F], F32)
        M["prelu"] = sb("prelu", [P, 1], F32)

        D = {}
        D["records"] = dram("records", [P * T, NR], F32)
        D["base"] = dram("base", [KS, CELLS], F32)
        D["starts"] = dram("starts", [CELLS], F32)
        D["tables"] = dram("tables", [3, NTAB * P], I32)
        D["nodes0"] = dram("nodes0", [NT * P, F], F32)
        D["nodes1"] = dram("nodes1", [NT * P * R, F], F32)
        D["count"] = dram("count", [CELLS + 1, P, W], F32)
        D["adj2"] = dram("adj2", [CELLS + 1, P, W], F32)
        D["rows"] = dram("rows", [4 * NT, P], F32)

        with ExitStack() as edges:
            M["edge"] = sb("edge", [EP, EC, NF], F32, edges)
            prepare(nc, A, M, D, edges, sem)
            sort_edges(nc, M, D, sem)
        with ExitStack() as passes:
            M["sorted"] = sb("sorted", [P, T, NR], F32, passes)
            M["cell_of"] = sb("cell_of", [1, T], I32, passes)
            M["offset_of"] = sb("offset_of", [1, T], I32, passes)
            M["nodes"] = sb("nodes", [P, NT, F], F32, passes)
            M["dinv"] = sb("dinv", [P, NT], F32, passes)
            chunk_tables(nc, A, M, D, sem)
            edge_pass(nc, A, M, D, sem, 0)
            relation_tables(nc, M, D, sem)
            edge_pass(nc, A, M, D, sem, 1)
        layer2(nc, A, M, D, sem)
        gcn(nc, A, M, D, sem)
        gat(nc, A, M, D, out, sem)


def prepare(nc, A, M, D, outer, sem):
    with ExitStack() as ctx:
        sb = lambda name, shape, dt: ctx.enter_context(nc.sbuf_tensor(name, shape, dt))
        ps = lambda name, shape, dt: ctx.enter_context(nc.psum_tensor(name, shape, dt))
        edge, x, h = M["edge"], M["x"], M["h"]
        M["iota_cell"] = outer.enter_context(nc.sbuf_tensor("iota_cell", [P, CW], F16))
        M["tri"] = outer.enter_context(nc.sbuf_tensor("tri", [P, P], BF16))
        M["rest"] = outer.enter_context(nc.sbuf_tensor("rest", [P, P], BF16))
        M["base_row"] = outer.enter_context(nc.sbuf_tensor("base_row", [1, KS, CW], F32))
        M["blank"] = outer.enter_context(nc.sbuf_tensor("blank", [P, T, NR], F32))
        src, dst, rel = (sb(n, [EP, EC], I32) for n in ("src_i", "dst_i", "rel_i"))
        w0, w1 = sb("w_raw", [EP, EC], F32), sb("w_rel", [EP, EC], F32)
        ti, tf = sb("t_i", [EP, EC], I32), sb("t_f", [EP, EC], F32)
        sbf, dbf = sb("src_tile", [EP, EC], F32), sb("dst_window", [EP, EC], F32)
        wb = sb("w_bf", [EP, EC], BF16)
        iota_i = sb("iota_i", [P, CW], I32)
        trif = sb("trif", [NT, NT], F32)
        xc, sq = M["hT"], sb("sq", [P, NT, F], F32)
        wbase = sb("wbase", [P, B, F], F32)
        wcomp = sb("wcomp", [P, R * B], F32)
        ohs, ohd = sb("hist_src", [EP, 2, G, NT], BF16), sb("hist_dst", [EP, 2, G, NW], BF16)
        hist = sb("hist", [NT, KS, NW], F32)
        tot, cum, cum2 = (sb(n, [NT, NW], F32) for n in ("tot", "cum", "cum2"))
        toti = sb("tot_i", [NT, NW], I32)
        acc = [ps(f"hist_ps{k}", [NT, NW], F32) for k in range(KS)]
        row_ps = ps("row_ps", [NT, 1], F32)

        loaded, x_cleared, x_in, weights_in = sem("loaded"), sem("x_cleared"), sem("x_in"), sem("weights_in")
        vec_in = sem("vec_in")
        made, sig_done, dve = sem("constants_made"), sem("sig_done"), sem("prep_dve")
        hist_ready, hist_used, row_ready, row_done = sem("hist_ready"), sem("hist_used"), sem("row_ready"), sem("row_done")
        starts_ready, starts_out, starts_in, blank_ready, blank_out = (
            sem(n) for n in ("starts_ready", "starts_out", "starts_in", "blank_ready", "blank_out"))
        var_ready, std_ready = sem("var_ready0"), sem("std_ready0")
        block = ctx.enter_context(nc.Block())

        @block.sync
        def _(sp):
            for t, n in ((src, "src"), (dst, "dst"), (rel, "edge_type_32"), (w0, "edge_weight")):
                sp.dma_start(t[:, :], A[n].rearrange("(p j) -> p j", p=EP)).then_inc(loaded, 16)
            sp.dma_start(w1[:, :], A["edge_weight1"].rearrange("(p j) o -> p (j o)", p=EP)).then_inc(loaded, 16)
            sp.wait_ge(x_cleared, 1)
            sp.dma_start(x[:, 0:NT - 1, :], A["x"][0:(NT - 1) * P, :].rearrange("(t p) f -> p t f", p=P)).then_inc(x_in, 16)
            sp.dma_start(x[0:TAIL, NT - 1, :], A["x"][(NT - 1) * P:N, :]).then_inc(x_in, 16)
            sp.dma_start(wbase[:, :, :], A["L1_gnn_weight"].rearrange("b d f -> d b f")).then_inc(weights_in, 16)
            sp.dma_start(wcomp[:, :], A["L1_gnn_w_comp"].rearrange("r b -> (r b)").partition_broadcast(P)).then_inc(weights_in, 16)
            for n, name in enumerate(VECS):
                sp.dma_start(M["vec"][:, n, :], A[name].partition_broadcast(P)).then_inc(vec_in, 16)
            sp.dma_start(M["prelu"][:, :], A["L2_gnn_prelu_a"].partition_broadcast(P)).then_inc(vec_in, 16)
            sp.wait_ge(vec_in, 16 * (len(VECS) + 1))
            sp.wait_ge(blank_ready, 2)
            sp.dma_start(D["records"].rearrange("(p c) f -> p (c f)", p=P), M["blank"][:, :, :].rearrange("p c f -> p (c f)")).then_inc(blank_out, 16)
            sp.wait_ge(starts_ready, 2)
            sp.dma_start(D["base"].rearrange("k (s d) -> s k d", d=NW), hist[:, :, :]).then_inc(starts_out, 16)
            sp.dma_start(D["starts"].rearrange("(s d) -> s d", d=NW), cum2[:, :]).then_inc(starts_out, 16)
            sp.wait_ge(starts_out, 32)
            sp.dma_start(M["base_row"][:, :, 0:CELLS], D["base"].rearrange("(o k) c -> o k c", o=1)).then_inc(starts_in, 16)
            sp.dma_start(M["start_row"][:, :], D["starts"].partition_broadcast(P)).then_inc(starts_in, 16)
            sp.wait_ge(starts_in, 32)
            sp.wait_ge(blank_out, 16)

        @block.gpsimd
        def _(pool):
            nc.gpsimd.iota(iota_i[:, :], [[1, CW]], base=0, channel_multiplier=0).then_inc(made, 1)
            nc.gpsimd.memset(M["ident"][:, :], 0.0).then_inc(made, 1)
            nc.gpsimd.memset(M["ones"][:, :], 1.0).then_inc(made, 1)
            nc.gpsimd.memset(M["tri"][:, :], 1.0).then_inc(made, 1)
            nc.gpsimd.memset(M["rest"][:, :], 1.0).then_inc(made, 1)
            nc.gpsimd.memset(M["zeros"][:, :], 0.0).then_inc(made, 1)
            pool.wait_ge(made, 6)
            nc.gpsimd.affine_select(out=M["ident"][:, :], in_=M["ident"][:, :], compare_op=ALU.not_equal, fill=1.0,
                                    base=0, pattern=[[-1, P]], channel_multiplier=1).then_inc(made, 1)
            nc.gpsimd.affine_select(out=M["tri"][:, :], in_=M["tri"][:, :], compare_op=ALU.is_gt, fill=0.0,
                                    base=0, pattern=[[1, P]], channel_multiplier=-1).then_inc(made, 1)
            nc.gpsimd.affine_select(out=M["rest"][:, :], in_=M["rest"][:, :], compare_op=ALU.is_ge, fill=0.0,
                                    base=0, pattern=[[-1, P]], channel_multiplier=1).then_inc(made, 1)
            nc.gpsimd.memset(M["blank"][:, :, :], 0.0).then_inc(blank_ready, 1)
            pool.wait_ge(blank_ready, 1)
            nc.gpsimd.memset(M["blank"][:, :, S_LOC:S_LOC + 1], -1.0).then_inc(blank_ready, 1)

        @block.scalar
        def _(act):
            act.wait_ge(loaded, 80)
            nc.scalar.activation(edge[:, :, W_SIG], w0[:, :], ACT.Sigmoid).then_inc(sig_done, 1)
            nc.scalar.activation(edge[:, :, W_RAW], w0[:, :], ACT.Copy).then_inc(sig_done, 1)
            nc.scalar.activation(edge[:, :, W_REL], w1[:, :], ACT.Copy).then_inc(sig_done, 1)
            nc.scalar.activation(edge[:, :, SRC], src[:, :], ACT.Copy).then_inc(sig_done, 1)
            nc.scalar.activation(edge[:, :, DST], dst[:, :], ACT.Copy).then_inc(sig_done, 1)
            root_of_variance(nc, act, var_ready, std_ready, M["stats"])

        @block.vector
        def _(v):
            link = linker(v, dve)
            nc.vector.memset(x[:, NT - 1, :], 0.0).then_inc(x_cleared, 1)
            link(nc.vector.memset(M["base_row"][:, :, CELLS:CW], 0.0))
            v.wait_ge(made, 9)
            link(nc.vector.tensor_copy(M["iota_cell"][:, :], iota_i[:, :]))
            link(nc.vector.tensor_copy(M["iota_w"][:, :], iota_i[:, 0:W]))
            link(nc.vector.tensor_copy(M["iota_f"][:, :], iota_i[:, 0:W]))
            link(nc.vector.tensor_copy(M["identb"][:, :], M["ident"][:, :]))
            link(nc.vector.tensor_copy(trif[:, :], M["tri"][0:NT, 0:NT]))
            v.wait_ge(loaded, 80)
            link(nc.vector.tensor_scalar(ti[:, :], src[:, :], 7, None, ALU.arith_shift_right))
            link(nc.vector.tensor_copy(sbf[:, :], ti[:, :]))
            link(nc.vector.tensor_scalar(ti[:, :], dst[:, :], 8, None, ALU.arith_shift_right))
            link(nc.vector.tensor_copy(dbf[:, :], ti[:, :]))
            link(nc.vector.scalar_tensor_tensor(edge[:, :, CELL], sbf[:, :], float(NW), dbf[:, :], ALU.mult, ALU.add))
            iota3 = M["iota_w"][0:EP, :].unsqueeze(1)
            with v.Fori(0, EC // (2 * G)) as i:
                for b in range(2):
                    col = i * (2 * G) + b * G
                    v.wait_ge(hist_used, i * 2 + (b + 1))
                    nc.vector.tensor_tensor(ohs[:, b, :, :], bcast(iota3[:, :, 0:NT], [EP, G, NT]),
                                            bcast(sbf[:, bass.ds(col, G)].unsqueeze(2), [EP, G, NT]),
                                            ALU.is_equal).then_inc(hist_ready, 1)
                    nc.vector.tensor_tensor(ohd[:, b, :, :], bcast(iota3[:, :, 0:NW], [EP, G, NW]),
                                            bcast(dbf[:, bass.ds(col, G)].unsqueeze(2), [EP, G, NW]),
                                            ALU.is_equal).then_inc(hist_ready, 1)
            v.wait_ge(hist_used, 2 + EC // G)
            for k in range(KS):
                link(nc.vector.tensor_copy(hist[:, k, :], acc[k][:, :]))
            link(nc.vector.tensor_tensor(tot[:, :], hist[:, 0, :], hist[:, 1, :], ALU.add))
            link(nc.vector.tensor_tensor(tot[:, :], tot[:, :], hist[:, 2, :], ALU.add))
            link(nc.vector.tensor_tensor(tot[:, :], tot[:, :], hist[:, 3, :], ALU.add))
            link(nc.vector.tensor_scalar(toti[:, :], tot[:, :], float(P - 1), None, ALU.add))
            link(nc.vector.tensor_scalar(toti[:, :], toti[:, :], 7, None, ALU.arith_shift_right))
            link(nc.vector.tensor_scalar(tot[:, :], toti[:, :], 1.0, None, ALU.max))
            a, b, step = cum, cum2, 1
            link(nc.vector.tensor_copy(a[:, :], tot[:, :]))
            while step < NW:
                link(nc.vector.tensor_copy(b[:, 0:step], a[:, 0:step]))
                link(nc.vector.tensor_tensor(b[:, step:NW], a[:, step:NW], a[:, 0:NW - step], ALU.add))
                a, b, step = b, a, 2 * step
            assert a is cum
            nc.vector.tensor_copy(toti[:, 0:1], toti[:, 0:1]).then_inc(row_ready, 1)
            v.wait_ge(row_done, 1)
            link(nc.vector.tensor_tensor(cum2[:, :], cum[:, :], tot[:, :], ALU.subtract))
            link(nc.vector.tensor_scalar(cum2[:, :], cum2[:, :], row_ps[:, 0:1], None, ALU.add))
            for k in range(1, KS - 1):
                link(nc.vector.tensor_tensor(hist[:, k, :], hist[:, k, :], hist[:, k - 1, :], ALU.add))
            for k in range(KS - 1, 0, -1):
                link(nc.vector.scalar_tensor_tensor(hist[:, k, :], cum2[:, :], float(P), hist[:, k - 1, :], ALU.mult, ALU.add))
            link(nc.vector.tensor_scalar(hist[:, 0, :], cum2[:, :], float(P), None, ALU.mult))
            nc.vector.tensor_copy(toti[:, 0:1], toti[:, 0:1]).then_inc(starts_ready, 2)
            link(nc.vector.tensor_scalar(ti[:, :], src[:, :], P - 1, None, ALU.bitwise_and))
            link(nc.vector.tensor_copy(edge[:, :, S_LOC], ti[:, :]))
            link(nc.vector.tensor_scalar(ti[:, :], dst[:, :], W - 1, None, ALU.bitwise_and))
            link(nc.vector.tensor_copy(edge[:, :, D_LOC], ti[:, :]))
            link(nc.vector.tensor_scalar(ti[:, :], dst[:, :], P - 1, None, ALU.bitwise_and))
            link(nc.vector.tensor_copy(edge[:, :, D_LO], ti[:, :]))
            link(nc.vector.tensor_scalar(ti[:, :], dst[:, :], 7, None, ALU.arith_shift_right))
            link(nc.vector.tensor_copy(edge[:, :, D_HI], ti[:, :]))
            link(nc.vector.scalar_tensor_tensor(edge[:, :, SRC_REL], src[:, :], float(R), rel[:, :], ALU.mult, ALU.add))
            v.wait_ge(sig_done, 5)
            link(nc.vector.tensor_copy(tf[:, :], edge[:, :, W_SIG]))
            for f in (W_A, W_B, W_C):
                link(nc.vector.tensor_copy(wb[:, :], tf[:, :]))
                link(nc.vector.tensor_copy(edge[:, :, f], wb[:, :]))
                link(nc.vector.tensor_tensor(tf[:, :], tf[:, :], edge[:, :, f], ALU.subtract))
            v.wait_ge(x_in, 32)
            layer_norm(nc, v, link, var_ready, std_ready, h[:, :, :], x[:, :, :], xc[:, :, :], sq[:, :, :], M["stats"])
            v.wait_ge(weights_in, 32)
            for b_ in range(B):
                for r in range(R):
                    c = wcomp[:, r * B + b_:r * B + b_ + 1]
                    if b_ == 0:
                        last = nc.vector.tensor_scalar(M["wrel"][:, r, :], wbase[:, 0, :], c, None, ALU.mult)
                    else:
                        last = nc.vector.scalar_tensor_tensor(M["wrel"][:, r, :], wbase[:, b_, :], c, M["wrel"][:, r, :],
                                                              ALU.mult, ALU.add)
                    if r == R - 1:
                        link(last)

        @block.tensor
        def _(pe):
            pe.wait_ge(made, 9)
            for k in range(KS):
                last = nc.tensor.matmul(acc[k][:, :], M["zeros"][:, 0:NT], M["zeros"][:, 0:NW], start=True, stop=True)
            last.then_inc(hist_used, 2)
            with pe.Fori(0, EC // (2 * G)) as i:
                for b in range(2):
                    pe.wait_ge(hist_ready, i * 4 + (2 * b + 2))
                    for k in range(G):
                        last = nc.tensor.matmul(acc[k % KS][:, :], ohs[:, b, k, :], ohd[:, b, k, :], start=False, stop=True,
                                                skip_group_check=True)
                    last.then_inc(hist_used, 1)
            pe.wait_ge(row_ready, 1)
            nc.tensor.matmul(row_ps[:, :], trif[:, :], cum[:, NW - 1:NW], start=True, stop=True).then_inc(row_done, 1)


def sort_edges(nc, M, D, sem):
    with ExitStack() as ctx:
        sb = lambda name, shape, dt: ctx.enter_context(nc.sbuf_tensor(name, shape, dt))
        ps = lambda name, shape, dt: ctx.enter_context(nc.psum_tensor(name, shape, dt))
        edge = M["edge"]
        NG = 4
        LOOPS = EC // (2 * G)
        stage = sb("stage", [EP, 2, G, NF], F32)
        oh = sb("oh_cell", [EP, NG, KS, CW], BF16)
        junk = sb("junk", [EP, KS, CW], BF16)
        lin, lin_i = sb("lin", [EP, 2, G], F32), sb("lin_i", [EP, 2, G], I32)
        lane, chunk = sb("lane", [EP, 2, G], I32), sb("chunk", [EP, 2, G], I32)
        pos = [sb(f"pos{b}", [EP, G], I32) for b in range(2)]
        ohl = sb("oh_dlow", [EP, 2, G, P], BF16)
        ohw = sb("oh_dhigh", [EP, 2, G, 4, NT], BF16)
        acc = [ps(f"rank_ps{k}", [EP, CW], F32) for k in range(KS)]
        deg = ps("deg_ps", [P, 4, NT], F32)
        stage_ready, oh_ready, tri_done, sel_done = sem("stage_ready"), sem("oh_ready"), sem("tri_done"), sem("sel_done")
        pos_ready, deg_ready, deg_used, dve = sem("pos_ready"), sem("deg_ready"), sem("deg_used"), sem("sort_dve")
        sent = [sem(f"sent{b}") for b in range(2)]
        fin, batch_seen = sem("deg_out"), sem("batch_seen")
        block = ctx.enter_context(nc.Block())

        @block.scalar
        def _(act):
            def stage_batch(i, b, first=False):
                if not first:
                    act.wait_ge(sent[b], i * (16 * G))
                    act.wait_ge(deg_used, i * 2 + (b + 1))
                nc.scalar.activation(stage[:, b, :, :], edge[:, bass.ds(i * (2 * G) + b * G, G), :],
                                     ACT.Copy).then_inc(stage_ready, 1)

            for b in range(2):
                stage_batch(0, b, first=True)
            with act.Fori(1, LOOPS) as i:
                for b in range(2):
                    stage_batch(i, b)

        @block.gpsimd
        def _(pool):
            with pool.Fori(0, LOOPS) as i:
                for b in range(2):
                    pool.wait_ge(pos_ready, i * 2 + (b + 1))
                    pool.sem_inc(batch_seen, 1)
                    for k in range(G):
                        nc.gpsimd.indirect_dma_start(D["records"][:, :],
                                                     bass.IndirectOffsetOnAxis(ap=pos[b][:, k:k + 1], axis=0),
                                                     stage[:, b, k, 0:NR], None).then_inc(sent[b], 16)
            for b in range(2):
                pool.wait_ge(sent[b], 16 * G * LOOPS)

        @block.vector
        def _(v):
            def one_hots(q):
                for k in range(KS):
                    last = nc.vector.tensor_scalar(oh[:, q, k, :], M["iota_cell"][0:EP, :],
                                                   stage[:, q // 2, (q % 2) * KS + k, CELL:CELL + 1], None, ALU.is_equal)
                last.then_inc(oh_ready, 1)

            nc.vector.memset(oh[:, NG - 1, :, :], 0.0).then_inc(sel_done, 1)
            with v.Fori(0, LOOPS) as i:
                for b in range(2):
                    v.wait_ge(stage_ready, i * 2 + (b + 1))
                    v.wait_ge(deg_used, i * 2 + (b + 1))
                    one = nc.vector.tensor_tensor(
                        ohw[:, b, :, 0, :], bcast(M["iota_w"][0:EP, 0:NT].unsqueeze(1), [EP, G, NT]),
                        bcast(stage[:, b, :, D_HI:D_HI + 1], [EP, G, NT]), ALU.is_equal)
                    one.then_inc(dve, 1)
                    for q in (2 * b, 2 * b + 1):
                        one_hots(q)
                    for k in range(G):
                        nc.vector.tensor_scalar(ohl[:, b, k, :], M["iota_w"][0:EP, 0:P], stage[:, b, k, D_LO:D_LO + 1],
                                                None, ALU.is_equal)
                    v.wait_ge(dve, i * 10 + (5 * b + 1))
                    for s in range(3):
                        last = nc.vector.tensor_tensor(ohw[:, b, :, 1 + s, :], ohw[:, b, :, 0, :],
                                                       bcast(stage[:, b, :, W_A + s:W_A + s + 1], [EP, G, NT]), ALU.mult)
                    last.then_inc(deg_ready, 1)
                    for q in (2 * b, 2 * b + 1):
                        v.wait_ge(tri_done, i * NG + (q + 1))
                        for k in range(KS):
                            last = nc.vector.tensor_tensor_reduce(
                                out=junk[:, k, :], in0=oh[:, q, k, :], in1=acc[k][:, :], scale=1.0, scalar=0.0,
                                op0=ALU.mult, op1=ALU.add, accum_out=lin[:, b, (q % 2) * KS + k:(q % 2) * KS + k + 1])
                        last.then_inc(sel_done, 1)
                    v.wait_ge(sel_done, i * NG + (2 * b + 3))
                    nc.vector.tensor_copy(lin_i[:, b, :], lin[:, b, :]).then_inc(dve, 1)
                    v.wait_ge(dve, i * 10 + (5 * b + 2))
                    nc.vector.tensor_scalar(lane[:, b, :], lin_i[:, b, :], P - 1, None, ALU.bitwise_and).then_inc(dve, 1)
                    nc.vector.tensor_scalar(chunk[:, b, :], lin_i[:, b, :], 7, None, ALU.arith_shift_right).then_inc(dve, 1)
                    v.wait_ge(dve, i * 10 + (5 * b + 4))
                    last = nc.vector.scalar_tensor_tensor(pos[b][:, :], lane[:, b, :], float(T), chunk[:, b, :],
                                                          ALU.mult, ALU.add)
                    last.then_inc(dve, 1)
                    v.wait_ge(dve, i * 10 + (5 * b + 5))
                    nc.vector.tensor_copy(lane[:, b, 0:1], chunk[:, b, 0:1]).then_inc(pos_ready, 1)
            v.wait_ge(deg_used, 2 + EC // G)
            nc.vector.tensor_copy(M["deg"][:, :, :], deg[:, :, :]).then_inc(fin, 1)
            v.wait_ge(fin, 1)

        @block.tensor
        def _(pe):
            for k in range(KS):
                nc.tensor.matmul(acc[k][:, :], M["ones"][0:1, 0:EP], M["base_row"][0:1, k, :], start=True, stop=True)
            nc.tensor.matmul(deg[:, :, :], M["zeros"][:, 0:P], M["zeros"][:, 0:4 * NT], start=True,
                             stop=True).then_inc(deg_used, 2)
            with pe.Fori(0, LOOPS) as i:
                for q in range(NG):
                    pe.wait_ge(oh_ready, i * NG + (q + 1))
                    pe.wait_ge(sel_done, i * NG + (q + 1))
                    for k in range(KS):
                        nc.tensor.matmul(acc[k][:, :], M["rest"][0:EP, 0:EP], oh[:, (q - 1) % NG, k, :],
                                         start=False, stop=True, skip_group_check=True)
                        last = nc.tensor.matmul(acc[k][:, :], M["tri"][0:EP, 0:EP], oh[:, q, k, :],
                                                start=False, stop=True, skip_group_check=True)
                    last.then_inc(tri_done, 1)
                    if q % 2:
                        b = q // 2
                        pe.wait_ge(deg_ready, i * 2 + (b + 1))
                        for k in range(G):
                            last = nc.tensor.matmul(deg[:, :, :], ohl[:, b, k, :], ohw[:, b, k, :, :],
                                                    start=False, stop=True, skip_group_check=True)
                        last.then_inc(deg_used, 1)


def spaces(nc, ctx, phase):
    def sb(name, shape, dt):
        return ctx.enter_context(nc.sbuf_tensor(f"{phase}_{name}", shape, dt))

    def ps(name, shape, dt):
        return ctx.enter_context(nc.psum_tensor(f"{phase}_{name}", shape, dt))
    return sb, ps


TB = 4
NTB = -(-NT // TB)


def transposes(nc, pe, h, ident, banks, done, copied):
    for m in range(NTB):
        if m >= 2:
            pe.wait_ge(copied, m - 1)
        for t in range(TB * m, min(TB * m + TB, NT)):
            last = nc.tensor.transpose(banks[m % 2][:, t % TB, :], h[:, t, :], ident)
        last.then_inc(done, 1)


def transposed_out(nc, act, hT, banks, done, copied):
    for m in range(NTB):
        n = min(TB, NT - TB * m)
        act.wait_ge(done, m + 1)
        nc.scalar.activation(hT[:, TB * m:TB * m + n, :], banks[m % 2][:, 0:n, :], ACT.Copy).then_inc(copied, 1)


def products(nc, pe, hT, weights, width, banks, done, taken):
    for t in range(NT):
        if t >= 2:
            pe.wait_ge(taken, t - 1)
        nc.tensor.matmul(banks[t % 2][:, 0:width], hT[:, t, :], weights, start=True, stop=True).then_inc(done, 1)


def chunk_tables(nc, A, M, D, sem):
    with ExitStack() as ctx:
        sb, ps = spaces(nc, ctx, "ct")
        c_i, c_f = sb("c_i", [P, 3, NTAB], I32), sb("c_f", [P, 3, NTAB], F32)
        cmp = sb("cmp", [P, NTAB, CELLS], BF16)
        cell, tile_of = sb("cell", [P, 3, NTAB], F32), sb("tile_of", [P, NTAB], F32)
        val, tab = sb("val", [P, NTAB], F32), sb("tab", [P, 3, NTAB], I32)
        same_i = sb("same_i", [P, T], I32)
        wt, wT, u = sb("w_sn", [P, F], F32), sb("w_snT", [P, F], F32), sb("u", [P, 1], F32)
        v0, sq2, sg = sb("v0", [P, 2], F32), sb("sq2", [P, 2], F32), sb("sg", [P, 2], F32)
        tps = [ps(f"tps{n}", [P, TB, P], F32) for n in range(2)]
        pps = [ps(f"pps{n}", [P, F], F32) for n in range(2)]
        small = ps("small", [P, 8], F32)
        wT_ps = ps("wT_ps", [P, F], F32)
        iota_done, rec_in, w_in, u_in = (sem(f"ct_{n}") for n in ("iota_done", "rec_in", "w_in", "u_in"))
        tab_ready, tab_out, tab_in, dve, root_in, root_out = (
            sem(f"ct_{n}") for n in ("tab_ready", "tab_out", "tab_in", "dve", "root_in", "root_out"))
        tr_done, tr_copied, pr_done, pr_taken, nodes_out, pe_step, dve_step = (
            sem(f"ct_{n}") for n in ("tr_done", "tr_copied", "pr_done", "pr_taken", "nodes_out", "pe_step", "dve_step"))
        block = ctx.enter_context(nc.Block())

        @block.sync
        def _(sp):
            sp.dma_start(wt[:, :], A["L0_gnn_weight"][:, :]).then_inc(w_in, 16)
            sp.dma_start(u[:, :], A["L0_gnn_u"].rearrange("(p o) -> p o", o=1)).then_inc(w_in, 16)
            sp.dma_start(M["sorted"][:, :, :].rearrange("p c f -> p (c f)"),
                         D["records"].rearrange("(p c) f -> p (c f)", p=P)).then_inc(rec_in, 16)
            sp.wait_ge(tab_ready, 1)
            for k in range(3):
                sp.dma_start(D["tables"][k].rearrange("(i p) -> p i", p=P), tab[:, k, :]).then_inc(tab_out, 16)
            sp.wait_ge(tab_out, 48)
            sp.dma_start(M["cell_of"][:, :], D["tables"][0:1, 0:T]).then_inc(tab_in, 16)
            sp.dma_start(M["offset_of"][:, :], D["tables"][1:2, 0:T]).then_inc(tab_in, 16)
            sp.dma_start(same_i[:, :], D["tables"][2, 0:T].partition_broadcast(P)).then_inc(tab_in, 16)
            sp.wait_ge(pr_taken, NT)
            sp.dma_start(D["nodes0"].rearrange("(t p) f -> p t f", p=P), M["nodes"][:, :, :]).then_inc(nodes_out, 16)
            sp.wait_ge(nodes_out, 16)
            sp.wait_ge(rec_in, 16)

        @block.gpsimd
        def _(pool):
            nc.gpsimd.iota(c_i[:, :, :], [[1, 3], [P, NTAB]], base=-1, channel_multiplier=1).then_inc(iota_done, 1)

        @block.scalar
        def _(act):
            act.wait_ge(root_in, 1)
            nc.scalar.activation(M["dinv"][:, :], M["dinv"][:, :], ACT.Sqrt).then_inc(root_out, 1)
            transposed_out(nc, act, M["hT"], tps, tr_done, tr_copied)
            for n in range(2):
                act.wait_ge(root_in, n + 2)
                nc.scalar.activation(sg[:, n:n + 1], small[:, 4 + n:5 + n], ACT.Sqrt).then_inc(root_out, 1)

        @block.vector
        def _(v):
            link = linker(v, dve)
            link(nc.vector.tensor_tensor(M["dinv"][:, :], M["deg"][:, 1, :], M["deg"][:, 2, :], ALU.add))
            link(nc.vector.tensor_tensor(M["dinv"][:, :], M["dinv"][:, :], M["deg"][:, 3, :], ALU.add))
            nc.vector.tensor_scalar(M["dinv"][:, :], M["dinv"][:, :], 1.0, None, ALU.add).then_inc(root_in, 1)
            v.wait_ge(root_out, 1)
            link(nc.vector.reciprocal(M["dinv"][:, :], M["dinv"][:, :]))
            v.wait_ge(pe_step, 2)
            link(nc.vector.tensor_copy(wT[:, :], wT_ps[:, :]))
            link(nc.vector.tensor_copy(v0[:, 0:1], small[:, 0:1]))
            link(nc.vector.tensor_tensor(sq2[:, 0:1], v0[:, 0:1], v0[:, 0:1], ALU.mult))
            nc.vector.tensor_copy(sq2[:, 1:2], sq2[:, 0:1]).then_inc(dve_step, 1)
            v.wait_ge(pe_step, 3)
            nc.vector.tensor_copy(val[:, 0:1], v0[:, 0:1]).then_inc(root_in, 1)
            v.wait_ge(root_out, 2)
            link(nc.vector.tensor_scalar(sg[:, 0:1], sg[:, 0:1], 1e-12, None, ALU.add))
            link(nc.vector.reciprocal(sg[:, 0:1], sg[:, 0:1]))
            nc.vector.tensor_tensor(v0[:, 0:1], v0[:, 0:1], sg[:, 0:1], ALU.mult).then_inc(dve_step, 1)
            v.wait_ge(pe_step, 4)
            link(nc.vector.tensor_copy(v0[:, 1:2], small[:, 1:2]))
            link(nc.vector.tensor_tensor(sq2[:, 0:1], v0[:, 1:2], v0[:, 1:2], ALU.mult))
            nc.vector.tensor_copy(sq2[:, 1:2], sq2[:, 0:1]).then_inc(dve_step, 1)
            v.wait_ge(pe_step, 5)
            nc.vector.tensor_copy(val[:, 0:1], v0[:, 0:1]).then_inc(root_in, 1)
            v.wait_ge(root_out, 3)
            link(nc.vector.tensor_scalar(sg[:, 1:2], sg[:, 1:2], 1e-12, None, ALU.add))
            link(nc.vector.tensor_copy(sq2[:, 0:1], small[:, 5:6]))
            link(nc.vector.reciprocal(sq2[:, 0:1], sq2[:, 0:1]))
            link(nc.vector.tensor_tensor(sg[:, 1:2], sg[:, 1:2], sq2[:, 0:1], ALU.mult))
            v.wait_ge(w_in, 32)
            nc.vector.tensor_scalar(wt[:, :], wt[:, :], sg[:, 1:2], None, ALU.mult).then_inc(dve_step, 1)
            v.wait_ge(iota_done, 1)
            link(nc.vector.tensor_copy(c_f[:, :, :], c_i[:, :, :]))
            for k in range(3):
                link(nc.vector.tensor_tensor(cmp[:, :, :], bcast(M["start_row"][:, :].unsqueeze(1), [P, NTAB, CELLS]),
                                             bcast(c_f[:, k, :].unsqueeze(2), [P, NTAB, CELLS]), ALU.is_le))
                link(nc.vector.tensor_reduce(cell[:, k, :], cmp[:, :, :], AX.X, ALU.add))
                if k == 1:
                    link(nc.vector.tensor_reduce(tile_of[:, :], cmp[:, :, :].rearrange("p i (s d) -> p i s d", d=NW)[:, :, :, 0],
                                                 AX.X, ALU.add))
            link(nc.vector.tensor_scalar(cell[:, 1, :], cell[:, 1, :], 1.0, None, ALU.subtract))
            link(nc.vector.scalar_tensor_tensor(val[:, :], cell[:, 1, :], 1.0, cell[:, 2, :], ALU.add, ALU.is_equal))
            link(nc.vector.tensor_scalar(c_f[:, 2, :], c_f[:, 1, :], float(T - 1), None, ALU.not_equal))
            link(nc.vector.tensor_tensor(val[:, :], val[:, :], c_f[:, 2, :], ALU.mult))
            link(nc.vector.tensor_scalar(c_f[:, 0, :], cell[:, 1, :], -1.0, float(CELLS), ALU.mult, ALU.add))
            link(nc.vector.tensor_tensor(val[:, :], val[:, :], c_f[:, 0, :], ALU.mult))
            link(nc.vector.tensor_tensor(tab[:, 0, :], val[:, :], cell[:, 1, :], ALU.add))
            link(nc.vector.scalar_tensor_tensor(val[:, :], tile_of[:, :], -float(NW), cell[:, 1, :], ALU.mult, ALU.add))
            link(nc.vector.tensor_scalar(tab[:, 1, :], val[:, :], float(NW), float(W), ALU.add, ALU.mult))
            link(nc.vector.scalar_tensor_tensor(tab[:, 2, :], cell[:, 1, :], 1.0, cell[:, 0, :], ALU.add, ALU.is_equal))
            nc.vector.tensor_copy(val[:, 0:1], tile_of[:, 0:1]).then_inc(tab_ready, 1)
            for t in range(NT):
                v.wait_ge(pr_done, t + 1)
                nc.vector.tensor_scalar(M["nodes"][:, t, :], pps[t % 2][:, :], M["dinv"][:, t:t + 1], None,
                                        ALU.mult).then_inc(pr_taken, 1)
            v.wait_ge(tab_in, 48)
            v.wait_ge(rec_in, 16)
            link(nc.vector.tensor_copy(M["sorted"][:, :, SAME], same_i[:, :]))

        @block.tensor
        def _(pe):
            pe.wait_ge(w_in, 32)
            nc.tensor.transpose(wT_ps[:, :], wt[:, :], M["ident"][:, :]).then_inc(pe_step, 1)
            nc.tensor.matmul(small[:, 0:1], wt[:, :], u[:, :], start=True, stop=True).then_inc(pe_step, 1)
            transposes(nc, pe, M["h"], M["ident"][:, :], tps, tr_done, tr_copied)
            pe.wait_ge(dve_step, 1)
            nc.tensor.matmul(small[:, 4:5], M["ones"][:, :], sq2[:, 0:1], start=True, stop=True).then_inc(pe_step, 1)
            pe.wait_ge(dve_step, 2)
            nc.tensor.matmul(small[:, 1:2], wT[:, :], v0[:, 0:1], start=True, stop=True).then_inc(pe_step, 1)
            pe.wait_ge(dve_step, 3)
            nc.tensor.matmul(small[:, 5:6], M["ones"][:, :], sq2[:, 0:1], start=True, stop=True).then_inc(pe_step, 1)
            pe.wait_ge(dve_step, 4)
            pe.wait_ge(tr_copied, NTB)
            products(nc, pe, M["hT"], wt[:, :], F, pps, pr_done, pr_taken)


def edge_pass(nc, A, M, D, sem, layer):
    with ExitStack() as ctx:
        sb, ps = spaces(nc, ctx, f"pass{layer}")
        s = lambda name: sem(f"{name}_{layer}")
        table = D["nodes0"] if layer == 0 else D["nodes1"]
        blocks = D["count"] if layer == 0 else D["adj2"]
        index, weight = (SRC, W_SIG) if layer == 0 else (SRC_REL, W_REL)
        NB = 4
        LOOPS = T // (NB * G)
        stage = sb("stage", [P, NB, G, NR], F32)
        idx = [sb(f"idx{b}", [P, G], I32) for b in range(NB)]
        rows = [sb(f"rows{b}", [P, G, F], F32) for b in range(NB)]
        od = sb("one_dst", [P, 2, G, W], F32)
        os = sb("one_src", [P, 2, G, P], F32)
        PAIRS = G // 2
        FREE = 2 + G
        blk = sb("blk", [P, 2 * G, W], F32)
        pair = sb("pair", [P, 2, 2, W], F32)
        xc, sq = M["hT"], M["nodes"]
        loop_w = sb("loop_w", [P, F], F32)
        sums = ps("sums", [P, 3584], F32)
        blk_ps = ps("blk_ps", [P, 2, W], F32)
        idx_ready, stage_ready, scaled, oh_ready, pe_done, blk_mm, pair_out, blk_taken, blk_free, seen = (
            s(n) for n in ("idx_ready", "stage_ready", "scaled", "oh_ready", "pe_done", "blk_mm", "pair_out", "blk_taken",
                           "blk_free", "seen"))
        gathered, written = [s(f"gathered{b}") for b in range(NB)], s("written")
        dve, var_ready, std_ready, loop_in = (s(n) for n in ("dve", "var_ready", "std_ready", "loop_in"))
        block = ctx.enter_context(nc.Block())

        @block.scalar
        def _(act):
            def stage_index(i, b):
                nc.scalar.activation(idx[b % NB][:, :], M["sorted"][:, bass.ds(i * (NB * G) + b * G, G), index],
                                     ACT.Copy).then_inc(idx_ready, 1)

            def stage_fields(i, b):
                nc.scalar.activation(stage[:, b % NB, :, :], M["sorted"][:, bass.ds(i * (NB * G) + b * G, G), :],
                                     ACT.Copy).then_inc(stage_ready, 1)

            def scale(b, k):
                return nc.scalar.activation(rows[b % NB][:, k, :], rows[b % NB][:, k, :], ACT.Copy,
                                            scale=stage[:, b % NB, k, weight:weight + 1])

            def body(i, last):
                for b in range(NB):
                    if not last:
                        stage_index(i, b + NB)
                    for j in range(PAIRS):
                        pairs = i * (NB * PAIRS) + (b * PAIRS + j)
                        act.wait_ge(blk_mm, pairs + 1)
                        act.wait_ge(blk_taken, i * (NB * G) + (b * G + 2 * j + FREE - 2))
                        nc.scalar.activation(pair[:, j % 2, :, :], blk_ps[:, :, :], ACT.Copy).then_inc(pair_out, 1)
                        if not (last and b == NB - 1):
                            if j == 0:
                                act.wait_ge(gathered[(b + 1) % NB], (i + (b + 1) // NB + 1) * (16 * G))
                                act.wait_ge(stage_ready, i * NB + (b + 2))
                            scale(b + 1, 2 * j)
                            scale(b + 1, 2 * j + 1).then_inc(scaled, 1)
                        if j == 1 and not (last and b >= NB - 2):
                            stage_fields(i, b + 2)

            act.sem_inc(pair_out, 1)
            for b in range(NB):
                stage_index(0, b)
            for b in range(2):
                stage_fields(0, b)
            act.wait_ge(gathered[0], 16 * G)
            act.wait_ge(stage_ready, 1)
            for j in range(PAIRS):
                scale(0, 2 * j)
                scale(0, 2 * j + 1).then_inc(scaled, 1)
            with act.Fori(0, LOOPS - 1) as i:
                body(i, False)
            body(LOOPS - 1, True)
            root_of_variance(nc, act, var_ready, std_ready, M["stats"])

        @block.gpsimd
        def _(pool):
            with pool.Fori(0, LOOPS) as i:
                for b in range(NB):
                    pool.wait_ge(idx_ready, i * NB + (b + 1))
                    pool.sem_inc(seen, 1)
                    pool.wait_ge(pe_done, i * NB + (b + 1))
                    pool.sem_inc(seen, 1)
                    for k in range(G):
                        nc.gpsimd.indirect_dma_start(rows[b][:, k, :], None, table[:, :],
                                                     bass.IndirectOffsetOnAxis(ap=idx[b][:, k:k + 1], axis=0)
                                                     ).then_inc(gathered[b], 16)

        @block.sync
        def _(sp):
            if layer == 1:
                sp.dma_start(loop_w[:, :], A["L1_gnn_loop_weight"][:, :]).then_inc(loop_in, 16)
            sp.sem_inc(blk_free, 2)
            with sp.Fori(0, LOOPS) as i:
                for b in range(NB):
                    cells = nc.values_load_multi_w_load_instructions(
                        M["cell_of"][0:1, bass.ds(i * (NB * G) + b * G, G)], engines=[mybir.EngineType.SP],
                        min_val=0, max_val=CELLS)[1]
                    for k in range(G):
                        sp.wait_ge(blk_taken, i * (NB * G) + (b * G + k + 1 + FREE))
                        sp.dma_start(blocks[bass.ds(cells[k], 1), :, :].rearrange("o p w -> p (o w)"),
                                     blk[:, (b % 2) * G + k, :], cond=cells[k] < CELLS).then_inc(written, 16)
                    sp.wait_ge(written, i * (NB * 16 * G) + (b + 1) * (16 * G))
                    sp.sem_inc(blk_free, 1)

        @block.vector
        def _(v):
            def one_hots(b, k):
                f = lambda n: stage[:, b % NB, k, n:n + 1]
                nc.vector.tensor_scalar(od[:, b % 2, k, :], M["iota_f"][:, :], f(D_LOC), None, ALU.is_equal)
                if layer == 0:
                    return nc.vector.tensor_scalar(os[:, b % 2, k, :], M["iota_f"][:, 0:P], f(S_LOC), None, ALU.is_equal)
                return nc.vector.tensor_scalar(os[:, b % 2, k, :], M["iota_f"][:, 0:P], f(S_LOC), f(W_RAW),
                                               ALU.is_equal, ALU.mult)

            def take(i, b, k):
                at = (b % 2) * G + k
                v.wait_ge(blk_taken, i * (NB * G) + (b * G + k + FREE))
                nc.vector.scalar_tensor_tensor(blk[:, at, :], blk[:, (at - 1) % (2 * G), :], stage[:, b, k, SAME:SAME + 1],
                                               pair[:, k // 2 % 2, k % 2, :], ALU.mult, ALU.add).then_inc(blk_taken, 1)

            def body(i, last):
                for b in range(NB):
                    v.wait_ge(blk_free, i * NB + (b + 1))
                    for j in range(PAIRS):
                        v.wait_ge(pair_out, i * (NB * PAIRS) + (b * PAIRS + j + 2))
                        take(i, b, 2 * j)
                        take(i, b, 2 * j + 1)
                        if last and b == NB - 1:
                            continue
                        if j == 0:
                            v.wait_ge(stage_ready, i * NB + (b + 2))
                        one_hots(b + 1, 2 * j)
                        one_hots(b + 1, 2 * j + 1).then_inc(oh_ready, 1)

            nc.vector.memset(blk[:, :, :], 0.0).then_inc(blk_taken, FREE)
            v.wait_ge(stage_ready, 1)
            for j in range(PAIRS):
                one_hots(0, 2 * j)
                one_hots(0, 2 * j + 1).then_inc(oh_ready, 1)
            with v.Fori(0, LOOPS - 1) as i:
                body(i, False)
            body(LOOPS - 1, True)
            v.wait_ge(pe_done, NB + NB * LOOPS)
            link = linker(v, dve)
            agg = sums[:, 0:NT * F].rearrange("p (t f) -> p t f", f=F)
            full = [P, NT, F]
            x, h = M["x"][:, :, :], M["h"][:, :, :]
            bias = bcast(M["vec"][:, B0 if layer == 0 else B1, :].unsqueeze(1), full)
            if layer == 0:
                link(nc.vector.tensor_tensor(xc[:, :, :], agg, M["nodes"][:, :, :], ALU.add))
                link(nc.vector.tensor_tensor(xc[:, :, :], xc[:, :, :], bcast(M["dinv"][:, :].unsqueeze(2), full), ALU.mult))
                link(nc.vector.tensor_tensor(xc[:, :, :], xc[:, :, :], bias, ALU.add))
                link(nc.vector.tensor_tensor(x, xc[:, :, :], x, ALU.add))
            else:
                link(nc.vector.tensor_tensor(xc[:, :, :], agg, bias, ALU.add))
                link(nc.vector.scalar_tensor_tensor(x, xc[:, :, :], 0.0, x, ALU.max, ALU.add))
            layer_norm(nc, v, link, var_ready, std_ready, h, x, xc[:, :, :], sq[:, :, :], M["stats"])

        @block.tensor
        def _(pe):
            for n in range(7):
                last = nc.tensor.matmul(sums[:, 512 * n:512 * n + 512], M["zeros"][:, 0:P], M["zeros"][:, :],
                                        start=True, stop=True)
            last.then_inc(pe_done, NB)
            if layer == 1:
                pe.wait_ge(loop_in, 16)
                for t in range(NT):
                    nc.tensor.matmul(sums[:, t * F:(t + 1) * F], M["hT"][:, t, :], loop_w[:, :], start=False, stop=True,
                                     skip_group_check=True)
            with pe.Fori(0, LOOPS) as i:
                for b in range(NB):
                    offs = nc.values_load_multi_w_load_instructions(
                        M["offset_of"][0:1, bass.ds(i * (NB * G) + b * G, G)], engines=[mybir.EngineType.PE],
                        min_val=0, max_val=(NW - 1) * W)[1]
                    p = b % 2
                    for j in range(PAIRS):
                        pe.wait_ge(pair_out, i * (NB * PAIRS) + (b * PAIRS + j + 1))
                        pe.wait_ge(oh_ready, i * (NB * PAIRS) + (b * PAIRS + j + 1))
                        for k in (2 * j, 2 * j + 1):
                            if layer == 0:
                                ins = nc.tensor.matmul(blk_ps[:, k % 2, :], os[:, p, k, :], od[:, p, k, :],
                                                       start=True, stop=True)
                            else:
                                for half in range(2):
                                    ins = nc.tensor.matmul(blk_ps[:, k % 2, half * P:half * P + P],
                                                           od[:, p, k, half * P:half * P + P], os[:, p, k, :],
                                                           start=True, stop=True)
                        ins.then_inc(blk_mm, 1)
                        pe.wait_ge(scaled, i * (NB * PAIRS) + (b * PAIRS + j + 1))
                        for k in (2 * j, 2 * j + 1):
                            for half in range(2):
                                ins = nc.tensor.matmul(sums[:, bass.ds(offs[k] + half * P, P)],
                                                       od[:, p, k, half * P:half * P + P], rows[b][:, k, :],
                                                       start=False, stop=True, skip_group_check=True)
                    ins.then_inc(pe_done, 1)


def relation_tables(nc, M, D, sem):
    with ExitStack() as ctx:
        sb, ps = spaces(nc, ctx, "rt")
        Q = R * F // 512
        y = sb("y", [P, 2, R * F], F32)
        tps = [ps(f"tps{n}", [P, TB, P], F32) for n in range(2)]
        yps = [ps(f"yps{n}", [P, 512], F32) for n in range(6)]
        tr_done, tr_copied, mm, taken_a, taken_v, stored = (
            sem(f"rt_{n}") for n in ("tr_done", "tr_copied", "mm", "taken_a", "taken_v", "stored"))
        wrel = M["wrel"][:, :, :].rearrange("p r f -> p (r f)")
        out_rows = D["nodes1"].rearrange("(t p r) f -> t p (r f)", p=P, r=R)
        block = ctx.enter_context(nc.Block())
        stores = [sem(f"rt_store{b}") for b in range(2)]

        @block.tensor
        def _(pe):
            transposes(nc, pe, M["h"], M["ident"][:, :], tps, tr_done, tr_copied)
            pe.wait_ge(tr_copied, NTB)
            for n in range(NT * Q):
                if n >= 6:
                    pe.wait_ge(taken_v if n % 2 else taken_a, (n - 6) // 2 + 1)
                nc.tensor.matmul(yps[n % 6][:, :], M["hT"][:, n // Q, :], wrel[:, (n % Q) * 512:(n % Q) * 512 + 512],
                                 start=True, stop=True).then_inc(mm, 1)

        def take(eng, copy, parity, taken):
            for t in range(NT):
                if t >= 2:
                    eng.wait_ge(stores[t % 2], 16 * (t // 2))
                for q in range(parity, Q, 2):
                    n = Q * t + q
                    eng.wait_ge(mm, n + 1)
                    copy(y[:, t % 2, q * 512:q * 512 + 512], yps[n % 6][:, :]).then_inc(taken, 1)

        @block.scalar
        def _(act):
            transposed_out(nc, act, M["hT"], tps, tr_done, tr_copied)
            take(act, lambda o, i: nc.scalar.activation(o, i, ACT.Copy), 0, taken_a)

        @block.vector
        def _(v):
            take(v, nc.vector.tensor_copy, 1, taken_v)

        @block.sync
        def _(sp):
            for t in range(NT):
                sp.wait_ge(taken_a, (t + 1) * Q // 2)
                sp.wait_ge(taken_v, (t + 1) * Q // 2)
                sp.dma_start(out_rows[t], y[:, t % 2, :]).then_inc(stores[t % 2], 16)
            for b in range(2):
                sp.wait_ge(stores[b], 16 * ((NT + 1 - b) // 2))


def layer2(nc, A, M, D, sem):
    with ExitStack() as ctx:
        sb, ps = spaces(nc, ctx, "l2")
        s = lambda n: sem(f"l2_{n}")
        w, wT = sb("w2", [P, F], F32), sb("w2T", [P, F], F32)
        tab = sb("tab2", [P, 2 * NW, F], F32)
        adj = [sb(f"adj{b}", [P, NW, W], F32) for b in range(2)]
        agg, xc, sq = (sb(n, [P, NT, F], F32) for n in ("agg2", "xc3", "sq3"))
        tps = [ps(f"tps{n}", [P, TB, P], F32) for n in range(2)]
        pps = [ps(f"pps{n}", [P, F], F32) for n in range(2)]
        aps = [ps(f"aps{n}", [P, F], F32) for n in range(2)]
        wT_ps = ps("wT_ps", [P, F], F32)
        w_in, wT_done, wT_copied, tr_done, tr_copied, pr_done, pr_taken = (
            s(n) for n in ("w_in", "wT_done", "wT_copied", "tr_done", "tr_copied", "pr_done", "pr_taken"))
        in_, summed, taken, dve, var_ready, std_ready = ([s("in0"), s("in1")], s("summed"), s("taken"), s("dve"),
                                                         s("var_ready"), s("std_ready"))
        cells = D["adj2"][0:CELLS].rearrange("(t c) p w -> t p c w", c=NW)
        block = ctx.enter_context(nc.Block())

        @block.sync
        def _(sp):
            sp.dma_start(w[:, :], A["L2_gnn_W"][:, :]).then_inc(w_in, 16)
            for t in range(2):
                sp.dma_start(adj[t][:, :, :], cells[t]).then_inc(in_[t], 16)
            with sp.Fori(0, NT // 2 - 1) as i:
                for b in range(2):
                    sp.wait_ge(summed, i * 2 + (b + 1))
                    sp.dma_start(adj[b][:, :, :],
                                 cells[bass.ds(i * 2 + (b + 2), 1)].rearrange("t p c w -> p (t c) w")).then_inc(in_[b], 16)
            sp.wait_ge(summed, NT - 2)
            sp.dma_start(adj[0][:, :, :], cells[NT - 1]).then_inc(in_[0], 16)
            sp.wait_ge(in_[0], 16 * (NT // 2 + 1))

        @block.scalar
        def _(act):
            act.wait_ge(wT_done, 1)
            nc.scalar.activation(wT[:, :], wT_ps[:, :], ACT.Copy).then_inc(wT_copied, 1)
            transposed_out(nc, act, M["hT"], tps, tr_done, tr_copied)
            root_of_variance(nc, act, var_ready, std_ready, M["stats"])

        @block.vector
        def _(v):
            link = linker(v, dve)
            link(nc.vector.memset(tab[:, NT, :], 0.0))
            for t in range(NT):
                v.wait_ge(pr_done, t + 1)
                nc.vector.tensor_copy(tab[:, t, :], pps[t % 2][:, :]).then_inc(pr_taken, 1)
            with v.Fori(0, NT // 2) as i:
                for b in range(2):
                    v.wait_ge(summed, i * 2 + (b + 1))
                    nc.vector.tensor_copy(agg[:, bass.ds(i * 2 + b, 1), :], aps[b][:, :].unsqueeze(1)).then_inc(taken, 1)
            v.wait_ge(summed, NT)
            link(nc.vector.tensor_copy(agg[:, NT - 1, :], aps[0][:, :]))
            v.wait_ge(taken, NT - 1)
            full = [P, NT, F]
            x, h = M["x"][:, :, :], M["h"][:, :, :]
            link(nc.vector.tensor_tensor(agg[:, :, :], agg[:, :, :], bcast(M["vec"][:, B2, :].unsqueeze(1), full), ALU.add))
            link(nc.vector.tensor_scalar(xc[:, :, :], agg[:, :, :], 0.0, M["prelu"][:, 0:1], ALU.min, ALU.mult))
            link(nc.vector.scalar_tensor_tensor(xc[:, :, :], agg[:, :, :], 0.0, xc[:, :, :], ALU.max, ALU.add))
            link(nc.vector.tensor_tensor(x, x, xc[:, :, :], ALU.add))
            layer_norm(nc, v, link, var_ready, std_ready, h, x, xc[:, :, :], sq[:, :, :], M["stats"])

        @block.tensor
        def _(pe):
            pe.wait_ge(w_in, 16)
            nc.tensor.transpose(wT_ps[:, :], w[:, :], M["ident"][:, :]).then_inc(wT_done, 1)
            transposes(nc, pe, M["h"], M["ident"][:, :], tps, tr_done, tr_copied)
            pe.wait_ge(tr_copied, NTB)
            pe.wait_ge(wT_copied, 1)
            products(nc, pe, M["hT"], wT[:, :], F, pps, pr_done, pr_taken)
            pe.wait_ge(pr_taken, NT)
            pe.wait_ge(dve, 1)

            def tile_sum(b):
                for n in range(2 * NW):
                    last = nc.tensor.matmul(aps[b][:, :], adj[b][:, n // 2, (n % 2) * P:(n % 2) * P + P], tab[:, n, :],
                                            start=(n == 0), stop=(n == 2 * NW - 1))
                last.then_inc(summed, 1)

            for b in range(2):
                pe.wait_ge(in_[b], 16)
                tile_sum(b)
            with pe.Fori(1, NT // 2) as i:
                for b in range(2):
                    pe.wait_ge(in_[b], i * 16 + 16)
                    pe.wait_ge(taken, i * 2 + (b - 1))
                    tile_sum(b)
            pe.wait_ge(in_[0], 16 * (NT // 2 + 1))
            pe.wait_ge(taken, NT - 2)
            tile_sum(0)


def gcn(nc, A, M, D, sem):
    with ExitStack() as ctx:
        sb, ps = spaces(nc, ctx, "gcn")
        s = lambda n: sem(f"gcn_{n}")
        w = sb("w3", [P, F], F32)
        tab = sb("tab3", [P, NT, F], F32)
        dinv = sb("dinv3", [P, NT], F32)
        cnt = [sb(f"cnt{b}", [P, NT, W], F32) for b in range(2)]
        agg, xc, sq = sb("agg3", [P, 2 * NW, F], F32), sb("xc4", [P, NT, F], F32), sb("sq4", [P, NT, F], F32)
        tps = [ps(f"tps{n}", [P, TB, P], F32) for n in range(2)]
        pps = [ps(f"pps{n}", [P, F], F32) for n in range(2)]
        aps = [[ps(f"aps{n}{h}", [P, F], F32) for h in range(2)] for n in range(2)]
        w_in, tr_done, tr_copied, pr_done, pr_taken, root_in, root_out = (
            s(n) for n in ("w_in", "tr_done", "tr_copied", "pr_done", "pr_taken", "root_in", "root_out"))
        in_, summed, taken, dve, var_ready, std_ready, sig = ([s("in0"), s("in1")], s("summed"), s("taken"), s("dve"),
                                                              s("var_ready"), s("std_ready"), s("sig"))
        cells = D["count"][0:CELLS].rearrange("(t c) p w -> c p t w", c=NW)
        block = ctx.enter_context(nc.Block())

        @block.sync
        def _(sp):
            sp.dma_start(w[:, :], A["L3_gnn_gcn_w"][:, :]).then_inc(w_in, 16)
            for g in range(2):
                sp.dma_start(cnt[g][:, :, :], cells[g]).then_inc(in_[g], 16)
            with sp.Fori(0, NW // 2 - 1) as i:
                for b in range(2):
                    sp.wait_ge(summed, i * 2 + (b + 1))
                    sp.dma_start(cnt[b][:, :, :], cells[bass.ds(i * 2 + (b + 2), 1)].rearrange("c p t w -> p (c t) w")).then_inc(in_[b], 16)
            sp.wait_ge(summed, NW - 2)
            sp.dma_start(cnt[0][:, :, :], cells[NW - 1]).then_inc(in_[0], 16)
            sp.wait_ge(in_[0], 16 * (NW // 2 + 1))

        @block.scalar
        def _(act):
            act.wait_ge(root_in, 1)
            nc.scalar.activation(dinv[:, :], dinv[:, :], ACT.Sqrt).then_inc(root_out, 1)
            transposed_out(nc, act, M["hT"], tps, tr_done, tr_copied)
            root_of_variance(nc, act, var_ready, std_ready, M["stats"])
            act.wait_ge(sig, 1)
            nc.scalar.activation(sq[:, :, :], xc[:, :, :], ACT.Sigmoid).then_inc(sig, 1)

        @block.vector
        def _(v):
            link = linker(v, dve)
            nc.vector.tensor_scalar(dinv[:, :], M["deg"][:, 0, :], 1.0, None, ALU.add).then_inc(root_in, 1)
            v.wait_ge(root_out, 1)
            link(nc.vector.reciprocal(dinv[:, :], dinv[:, :]))
            for t in range(NT):
                v.wait_ge(pr_done, t + 1)
                nc.vector.tensor_scalar(tab[:, t, :], pps[t % 2][:, :], dinv[:, t:t + 1], None, ALU.mult).then_inc(pr_taken, 1)

            with v.Fori(0, NW // 2) as i:
                for b in range(2):
                    v.wait_ge(summed, i * 2 + (b + 1))
                    for h in range(2):
                        nc.vector.tensor_copy(agg[:, bass.ds(i * 4 + (2 * b + h), 1), :], aps[b][h][:, :].unsqueeze(1)).then_inc(taken, 1)
            v.wait_ge(summed, NW)
            link(nc.vector.tensor_copy(agg[:, NT - 1, :], aps[0][0][:, :]))
            v.wait_ge(taken, 2 * (NW - 1))
            full = [P, NT, F]
            g = agg[:, 0:NT, :]
            h = M["h"][:, :, :]
            vec = lambda n: bcast(M["vec"][:, n, :].unsqueeze(1), full)
            link(nc.vector.tensor_tensor(g, g, tab[:, :, :], ALU.add))
            link(nc.vector.tensor_tensor(g, g, bcast(dinv[:, :].unsqueeze(2), full), ALU.mult))
            link(nc.vector.tensor_tensor(g, g, vec(B_GCN), ALU.add))
            layer_norm(nc, v, link, var_ready, std_ready, h, g, xc[:, :, :], sq[:, :, :], M["stats"], relu=False)
            link(nc.vector.tensor_tensor(h, h, vec(GAMMA), ALU.mult))
            nc.vector.tensor_tensor(xc[:, :, :], h, vec(BETA), ALU.add).then_inc(sig, 1)
            v.wait_ge(sig, 2)
            link(nc.vector.tensor_tensor(h, xc[:, :, :], sq[:, :, :], ALU.mult))

        @block.tensor
        def _(pe):
            transposes(nc, pe, M["h"], M["ident"][:, :], tps, tr_done, tr_copied)
            pe.wait_ge(tr_copied, NTB)
            pe.wait_ge(w_in, 16)
            products(nc, pe, M["hT"], w[:, :], F, pps, pr_done, pr_taken)
            pe.wait_ge(pr_taken, NT)

            def window_sum(b):
                for h in range(2):
                    for t in range(NT):
                        last = nc.tensor.matmul(aps[b][h][:, :], cnt[b][:, t, h * P:h * P + P], tab[:, t, :],
                                                start=(t == 0), stop=(t == NT - 1))
                last.then_inc(summed, 1)

            for b in range(2):
                pe.wait_ge(in_[b], 16)
                window_sum(b)
            with pe.Fori(1, NW // 2) as i:
                for b in range(2):
                    pe.wait_ge(in_[b], i * 16 + 16)
                    pe.wait_ge(taken, i * 4 + (2 * b - 2))
                    window_sum(b)
            pe.wait_ge(in_[0], 16 * (NW // 2 + 1))
            pe.wait_ge(taken, 2 * (NW - 2))
            window_sum(0)


def gat(nc, A, M, D, out, sem):
    with ExitStack() as ctx:
        sb, ps = spaces(nc, ctx, "gat")
        s = lambda n: sem(f"gat_{n}")
        H = 2
        AW = H * F + 2 * H
        w = sb("w", [P, AW], F32)
        att = sb("att", [P, 2 * H, F], F32)
        haug = sb("haug", [P, NT, H, F + 1], F32)
        acol = sb("acol", [P, 2 * H, NT], F32)
        acol5 = sb("acol5", [P, NT, H], F32)
        arow_s, arow = sb("arow_s", [H * NT, P], F32), sb("arow", [P, H, NT * P], F32)
        cnt = [sb(f"cnt{b}", [P, NT, W], F32) for b in range(2)]
        pen = sb("pen", [P, NT, W], BF16)
        mx, m, e = sb("mx", [P, 2, H, NTB], F32), sb("m", [P, 2, H], F32), sb("e", [P, 2, H], F32)
        r12 = sb("r12", [P, 2, 2, H], F32)
        diag = sb("diag", [P, 2, 2, H, P], F32)
        rows = sb("rows", [P, 2, H, W], F32)
        t2, z, ex, pm = (sb(n, [P, 2, H, W], F32) for n in ("t2", "z", "ex", "pm"))
        junk = [t[:, :, :, :].rearrange("p b h w -> p (b h w)").bitcast(BF16).rearrange("p (n c) -> p n c", n=2 * H)
                for t in (z, ex)]
        rec = sb("rec", [P, 2, H], F32)
        part = sb("part", [P, 2, F], F32)
        tps = [ps(f"tps{n}", [P, 512], F32) for n in range(2)]
        rps = [ps(f"rps{n}", [P, H, W], F32) for n in range(2)]
        aps = [ps(f"aps{n}", [P, 512], F32) for n in range(2)]
        ops = [t[:, 0:H * (F + 1)].rearrange("p (h f) -> p h f", h=H) for t in aps]
        w_in, wv, tr_done, tr_copied, pr_done, pr_taken, at_done, at_copied, row_out, row_in, dve = (
            s(n) for n in ("w_in", "wv", "tr_done", "tr_copied", "pr_done", "pr_taken", "at_done", "at_copied", "row_out",
                           "row_in", "dve"))
        in_, pen_ready, pt_done, pt_taken, diag_ready, rows_mm, rows_ready, group_done = (
            [s("in0"), s("in1")], s("pen_ready"), s("pt_done"), s("pt_taken"), s("diag_ready"), s("rows_mm"), s("rows_ready"),
            s("group_done"))
        t2_done, z_done, ex_done, pm_done, mm_done, chain, self_added = (
            s(n) for n in ("t2_done", "z_done", "ex_done", "pm_done", "mm_done", "chain", "self_added"))
        var_ready, std_ready, sig, o_ready, stored = s("var_ready"), s("std_ready"), s("sig"), s("o_ready"), s("stored")
        acc_g = M["wrel"][:, 0:NT, :]
        cells = D["count"][0:CELLS].rearrange("(t c) p w -> c p t w", c=NW)
        tb16 = [t[:, :].bitcast(BF16).rearrange("p (h c) -> p h c", h=2) for t in tps]
        seen = s("seen")
        block = ctx.enter_context(nc.Block())

        @block.sync
        def _(sp):
            sp.dma_start(w[:, 0:H * F], A["L3_gnn_gat_w"][:, :]).then_inc(w_in, 16)
            for n, name in enumerate(("L3_gnn_att_src", "L3_gnn_att_dst")):
                sp.dma_start(att[:, n * H:n * H + H, :].rearrange("p h f -> p (h f)"),
                             A[name].rearrange("h f -> (h f)").partition_broadcast(P)).then_inc(w_in, 16)
            for g in range(2):
                sp.dma_start(cnt[g][:, :, :], cells[g]).then_inc(in_[g], 16)
            sp.wait_ge(at_copied, 1)
            sp.dma_start(D["rows"][0:H * NT, :], arow_s[:, :]).then_inc(row_out, 16)
            sp.wait_ge(row_out, 16)
            sp.dma_start(arow[:, :, :].rearrange("p h n -> p (h n)"),
                         D["rows"][0:H * NT, :].rearrange("a n -> (a n)").partition_broadcast(P)).then_inc(row_in, 16)
            with sp.Fori(0, NW // 2 - 1) as i:
                for b in range(2):
                    sp.wait_ge(group_done, i * 2 + (b + 1))
                    sp.dma_start(cnt[b][:, :, :], cells[bass.ds(i * 2 + (b + 2), 1)].rearrange("c p t w -> p (c t) w")).then_inc(in_[b], 16)
            sp.wait_ge(group_done, NW - 2)
            sp.dma_start(cnt[0][:, :, :], cells[NW - 1]).then_inc(in_[0], 16)
            sp.wait_ge(o_ready, 1)
            sp.dma_start(out[0:(NT - 1) * P, :].rearrange("(t p) f -> p t f", p=P), M["x"][:, 0:NT - 1, :]).then_inc(stored, 16)
            sp.dma_start(out[(NT - 1) * P:N, :], M["x"][0:TAIL, NT - 1, :]).then_inc(stored, 16)
            sp.wait_ge(stored, 32)

        @block.scalar
        def _(act):
            transposed_out(nc, act, M["hT"], [t[:, :].rearrange("p (t c) -> p t c", t=TB) for t in tps], tr_done, tr_copied)
            for t in range(NT):
                act.wait_ge(pr_done, t + 1)
                nc.scalar.activation(haug[:, t, :, 0:F], aps[t % 2][:, 0:H * F].rearrange("p (h f) -> p h f", h=H), ACT.Copy)
                nc.scalar.activation(acol[:, :, t], aps[t % 2][:, H * F:AW], ACT.Copy).then_inc(pr_taken, 1)
            act.wait_ge(at_done, 1)
            nc.scalar.activation(arow_s[:, :], rps[0][0:H * NT, 0, 0:P], ACT.Copy).then_inc(at_copied, 1)
            act.wait_ge(wv, 3)

            def window(g, b, nh):
                n = nh * P
                act.wait_ge(rows_mm, g + 1)
                for q in range(2):
                    ins = nc.scalar.activation(rows[:, q, :, 0:n], rps[q][:, :, 0:n], ACT.Copy)
                ins.then_inc(rows_ready, 1)
                act.wait_ge(rows_ready, g + 1)

                def slope(t):
                    if t >= 2:
                        act.wait_ge(z_done, g * NT + (t - 1))
                    for h in range(H):
                        ins = nc.scalar.activation(t2[:, t % 2, h, 0:n], rows[:, 1, h, 0:n], ACT.Identity,
                                                   bias=acol5[:, t, h:h + 1])
                    ins.then_inc(t2_done, 1)

                slope(0)
                for t in range(NT):
                    if t + 1 < NT:
                        slope(t + 1)
                    act.wait_ge(z_done, g * NT + (t + 1))
                    if t >= 2:
                        act.wait_ge(pm_done, g * NT + (t - 1))
                    nc.scalar.activation(ex[:, t % 2, :, 0:n], z[:, t % 2, :, 0:n], ACT.Exp).then_inc(ex_done, 1)

            with act.Fori(0, NW // 2) as i:
                for b in range(2):
                    window(i * 2 + b, b, 2)
            window(NW - 1, 0, 1)
            root_of_variance(nc, act, var_ready, std_ready, M["stats"])
            act.wait_ge(sig, 1)
            nc.scalar.activation(acc_g[:, :, :], M["hT"][:, :, :], ACT.Sigmoid).then_inc(sig, 1)

        @block.vector
        def _(v):
            link = linker(v, dve)
            v.wait_ge(w_in, 48)
            for n in range(2 * H):
                h = n % H
                link(nc.vector.tensor_tensor(part[:, 0, :], w[:, h * F:(h + 1) * F], att[:, n, :], ALU.mult))
                link(nc.vector.tensor_reduce(w[:, H * F + n:H * F + n + 1], part[:, 0, :], AX.X, ALU.add))
            nc.vector.memset(haug[:, :, :, F:F + 1], 1.0).then_inc(wv, 1)
            v.wait_ge(wv, 1)
            nc.vector.memset(mx[:, :, :, :], 0.0).then_inc(wv, 1)
            v.wait_ge(pr_taken, NT)
            nc.vector.tensor_scalar(acol5[:, :, :], acol[:, 0:H, :].rearrange("p h t -> p t h"), 0.2, None, ALU.mult).then_inc(wv, 1)
            v.wait_ge(row_in, 16)

            def window(g, b, nh, base):
                step = [0]

                def order(ins):
                    step[0] += 1
                    ins.then_inc(chain, 1)
                    v.wait_ge(chain, base + step[0])

                n = nh * P
                c = cnt[b]
                v.wait_ge(in_[b], g * 8 + (16 - 8 * b))
                for h in range(nh):
                    tile = g * 2 + h
                    own = c[:, bass.ds(tile, 1), h * P:(h + 1) * P]
                    order(nc.vector.tensor_tensor(own, own, M["ident"][:, :].unsqueeze(1), ALU.add))
                nc.vector.tensor_scalar(pen[:, :, 0:n], c[:, :, 0:n], 0.0, -1e30, ALU.is_equal, ALU.mult).then_inc(pen_ready, 1)
                for k in range(NTB):
                    tiles = min(TB, NT - TB * k)
                    v.wait_ge(pt_done, g * NTB + (k + 1))
                    v.sem_inc(seen, 1)
                    for h in range(nh):
                        for a in range(H):
                            ins = nc.vector.tensor_tensor_reduce(
                                out=junk[k % 2][:, h * H + a, 0:tiles * P], in0=tb16[k % 2][:, h, 0:tiles * P],
                                in1=arow[:, a, TB * P * k:TB * P * k + tiles * P], scale=1.0, scalar=-3e38,
                                op0=ALU.add, op1=ALU.max, accum_out=mx[:, h, a, k:k + 1])
                    ins.then_inc(pt_taken, 1)
                v.wait_ge(pt_taken, g * NTB + NTB)
                order(nc.vector.tensor_reduce(m[:, 0:nh, :], mx[:, 0:nh, :, :], AX.X, ALU.max))
                adst = acol[:, H:2 * H, bass.ds(g * 2, nh)].rearrange("p a t -> p t a")
                order(nc.vector.tensor_tensor(e[:, 0:nh, :], m[:, 0:nh, :], adst, ALU.add))
                order(nc.vector.scalar_tensor_tensor(m[:, 0:nh, :], e[:, 0:nh, :], 0.2, e[:, 0:nh, :], ALU.mult, ALU.max))
                order(nc.vector.tensor_tensor(r12[:, 0, 0:nh, :], adst, m[:, 0:nh, :], ALU.subtract))
                order(nc.vector.scalar_tensor_tensor(r12[:, 1, 0:nh, :], adst, 0.2, m[:, 0:nh, :], ALU.mult, ALU.subtract))
                for q in range(2):
                    for h in range(nh):
                        for a in range(H):
                            ins = nc.vector.tensor_scalar(diag[:, q, h, a, :], M["ident"][:, :], r12[:, q, h, a:a + 1], None, ALU.mult)
                ins.then_inc(diag_ready, 1)
                v.wait_ge(rows_ready, g + 1)

                def leaky(t):
                    v.wait_ge(t2_done, g * NT + (t + 1))
                    if t >= 2:
                        v.wait_ge(ex_done, g * NT + (t - 1))
                    for a in range(H):
                        ins = nc.vector.scalar_tensor_tensor(z[:, t % 2, a, 0:n], rows[:, 0, a, 0:n], acol[:, a, t:t + 1],
                                                             t2[:, t % 2, a, 0:n], ALU.add, ALU.max)
                    ins.then_inc(z_done, 1)

                leaky(0)
                for t in range(NT):
                    if t + 1 < NT:
                        leaky(t + 1)
                    v.wait_ge(ex_done, g * NT + (t + 1))
                    if t >= 2:
                        v.wait_ge(mm_done, g * NT + (t - 1))
                    nc.vector.tensor_tensor(pm[:, t % 2, :, 0:n], ex[:, t % 2, :, 0:n],
                                            bcast(c[:, t:t + 1, 0:n], [P, H, n]), ALU.mult).then_inc(pm_done, 1)
                v.wait_ge(mm_done, g * NT + NT)
                for h in range(nh):
                    ins = nc.vector.reciprocal(rec[:, h, :], ops[h][:, :, F])
                order(ins)
                for h in range(nh):
                    ins = nc.vector.tensor_scalar(part[:, h, :], ops[h][:, 0, 0:F], rec[:, h, 0:1], None, ALU.mult)
                order(ins)
                for h in range(nh):
                    ins = nc.vector.scalar_tensor_tensor(acc_g[:, bass.ds(g * 2 + h, 1), :], ops[h][:, 1:2, 0:F], rec[:, h, 1:2],
                                                         part[:, h:h + 1, :], ALU.mult, ALU.add)
                ins.then_inc(group_done, 1)

            with v.Fori(0, NW // 2) as i:
                for b in range(2):
                    window(i * 2 + b, b, 2, i * 18 + 9 * b)
            window(NW - 1, 0, 1, 9 * (NW - 1))
            v.wait_ge(group_done, NW)
            full = [P, NT, F]
            g3, h, xc, sq = acc_g[:, :, :], M["h"][:, :, :], M["hT"][:, :, :], haug[:, :, 0, 0:F]
            vec = lambda n: bcast(M["vec"][:, n, :].unsqueeze(1), full)
            link(nc.vector.scalar_tensor_tensor(g3, g3, 0.5, vec(B_GAT), ALU.mult, ALU.add))
            layer_norm(nc, v, link, var_ready, std_ready, h, g3, xc, sq, M["stats"], relu=False)
            link(nc.vector.tensor_tensor(h, h, vec(GAMMA), ALU.mult))
            nc.vector.tensor_tensor(xc, h, vec(BETA), ALU.add).then_inc(sig, 1)
            v.wait_ge(sig, 2)
            link(nc.vector.tensor_tensor(h, xc, g3, ALU.mult))
            nc.vector.tensor_tensor(M["x"][:, :, :], M["x"][:, :, :], h, ALU.add).then_inc(o_ready, 1)

        @block.tensor
        def _(pe):
            transposes(nc, pe, M["h"], M["ident"][:, :], [t[:, :].rearrange("p (t c) -> p t c", t=TB) for t in tps],
                       tr_done, tr_copied)
            pe.wait_ge(tr_copied, NTB)
            pe.wait_ge(wv, 1)
            for t in range(NT):
                if t >= 2:
                    pe.wait_ge(pr_taken, t - 1)
                nc.tensor.matmul(aps[t % 2][:, 0:AW], M["hT"][:, t, :], w[:, :], start=True, stop=True).then_inc(pr_done, 1)
            pe.wait_ge(pr_taken, NT)
            nc.tensor.transpose(rps[0][0:H * NT, 0, 0:P], acol[:, 0:H, :].rearrange("p h t -> p (h t)"), M["ident"][:, :]).then_inc(at_done, 1)

            def window(g, b, nh):
                n = nh * P
                pe.wait_ge(pen_ready, g + 1)
                for k in range(NTB):
                    if k >= 2:
                        pe.wait_ge(pt_taken, g * NTB + (k - 1))
                    for t in range(TB * k, min(TB * k + TB, NT)):
                        for h in range(nh):
                            ins = nc.tensor.transpose(tb16[k % 2][:, h, (t % TB) * P:(t % TB) * P + P],
                                                      pen[:, t, h * P:(h + 1) * P], M["identb"][:, :])
                    ins.then_inc(pt_done, 1)
                pe.wait_ge(diag_ready, g + 1)
                for q in range(2):
                    for a in range(H):
                        for h in range(nh):
                            ins = nc.tensor.matmul(rps[q][:, a, h * P:(h + 1) * P], M["ones"][:, :], diag[:, q, h, a, :],
                                                   start=True, stop=True)
                ins.then_inc(rows_mm, 1)
                for t in range(NT):
                    pe.wait_ge(pm_done, g * NT + (t + 1))
                    for h in range(nh):
                        for a in range(H):
                            ins = nc.tensor.matmul(ops[h][:, a, :], pm[:, t % 2, a, h * P:(h + 1) * P], haug[:, t, a, :],
                                                   start=(t == 0 and a == 0), stop=True, skip_group_check=True)
                    ins.then_inc(mm_done, 1)

            with pe.Fori(0, NW // 2) as i:
                for b in range(2):
                    window(i * 2 + b, b, 2)
            window(NW - 1, 0, 1)


NAMES = ['x', 'src', 'dst', 'edge_type_32', 'edge_weight', 'edge_weight1', 'L0_gnn_weight', 'L0_gnn_bias', 'L0_gnn_u',
         'L1_gnn_weight', 'L1_gnn_w_comp', 'L1_gnn_loop_weight', 'L1_gnn_h_bias', 'L2_gnn_W', 'L2_gnn_bias',
         'L2_gnn_prelu_a', 'L3_gnn_gcn_w', 'L3_gnn_gcn_b', 'L3_gnn_gat_w', 'L3_gnn_att_src', 'L3_gnn_att_dst',
         'L3_gnn_gat_b', 'L3_gnn_ln_gamma', 'L3_gnn_ln_beta']


def kernel(**inputs):
    import numpy as _np
    import concourse.bacc as _bacc
    from concourse.bass_utils import run_bass_kernel_spmd as _run

    nc = _bacc.Bacc("TRN2", target_bir_lowering=False, num_devices=1)
    arrays, args = {}, {}
    for name in NAMES:
        a = _np.ascontiguousarray(inputs[name])
        arrays["in_" + name] = a
        args[name] = nc.dram_tensor("in_" + name, a.shape, mybir.dt.from_np(a.dtype), kind="ExternalInput").ap()
    out = nc.dram_tensor("out_0", (N, F), F32, kind="ExternalOutput").ap()
    program(nc, args, out)
    r = _run(nc, [arrays], core_ids=[0])
    return r.results[0]["out_0"]
```

```python
import concourse.bass as bass
from concourse import mybir
from contextlib import ExitStack

F32 = mybir.dt.float32
BF16 = mybir.dt.bfloat16
F16 = mybir.dt.float16
I32 = mybir.dt.int32
ALU = mybir.AluOpType
ACT = mybir.ActivationFunctionType
AX = mybir.AxisListType

P = 128
N = 3125
F = 128
E = 100000
R = 32
B = 8
NT = -(-N // P)
TAIL = N - (NT - 1) * P
W = 2 * P
NW = -(-N // W)
CELLS = NT * NW
CW = CELLS + (-CELLS) % 8
EP = 125
EC = E // EP
G = 8
KS = 4
T = -(-((E + CELLS * P) // P) // (4 * G)) * 4 * G
NR = 8
(S_LOC, D_LOC, W_SIG, W_RAW, W_REL, SRC, SRC_REL, DST, CELL, D_LO, D_HI, W_A, W_B, W_C, NF) = range(15)
SAME = DST
EPS = 1e-05


VECS = ["L0_gnn_bias", "L1_gnn_h_bias", "L2_gnn_bias", "L3_gnn_gcn_b", "L3_gnn_gat_b", "L3_gnn_ln_gamma", "L3_gnn_ln_beta"]
(B0, B1, B2, B_GCN, B_GAT, GAMMA, BETA) = range(len(VECS))
NTAB = -(-T // P)


def linker(eng, sem, base=0):
    count = [0]

    def link(ins):
        count[0] += 1
        ins.then_inc(sem, 1)
        eng.wait_ge(sem, base + count[0])
        return count[0]
    return link


def bcast(ap, shape):
    return ap.broadcast_to(shape)


def layer_norm(nc, v, link, var_ready, std_ready, out, x, scratch, sq, st, relu=True, nth=1):
    full = [P, NT, F]
    mean, rstd = st[:, 0, :], st[:, 1, :]
    link(nc.vector.tensor_reduce(mean, x, AX.X, ALU.add))
    link(nc.vector.tensor_scalar(mean, mean, 1.0 / F, None, ALU.mult))
    link(nc.vector.tensor_tensor(scratch, x, bcast(mean.unsqueeze(2), full), ALU.subtract))
    link(nc.vector.tensor_tensor(sq, scratch, scratch, ALU.mult))
    link(nc.vector.tensor_reduce(rstd, sq, AX.X, ALU.add))
    nc.vector.tensor_scalar(rstd, rstd, 1.0 / F, EPS, ALU.mult, ALU.add).then_inc(var_ready, 1)
    v.wait_ge(std_ready, nth)
    link(nc.vector.reciprocal(rstd, rstd))
    link(nc.vector.tensor_tensor(out, scratch, bcast(rstd.unsqueeze(2), full), ALU.mult))
    if relu:
        link(nc.vector.tensor_scalar(out, out, 0.0, None, ALU.max))


def root_of_variance(nc, act, var_ready, std_ready, st, nth=1):
    act.wait_ge(var_ready, nth)
    nc.scalar.activation(st[:, 1, :], st[:, 1, :], ACT.Sqrt).then_inc(std_ready, 1)


def program(nc, A, out):
    with ExitStack() as ctx:
        ctx.enter_context(nc.allow_non_contiguous_dma(reason="small tables"))
        sb = lambda name, shape, dt, c=ctx: c.enter_context(nc.sbuf_tensor(name, shape, dt))
        ps = lambda name, shape, dt, c=ctx: c.enter_context(nc.psum_tensor(name, shape, dt))
        sem = lambda name: ctx.enter_context(nc.semaphore(name))
        dram = lambda name, shape, dt: nc.dram_tensor(name, shape, dt).ap()

        M = {"seen": sem("seen")}
        M["x"] = sb("x", [P, NT, F], F32)
        M["h"] = sb("h", [P, NT, F], F32)
        M["ident"] = sb("ident", [P, P], F32)
        M["identb"] = sb("identb", [P, P], BF16)
        M["iota_w"] = sb("iota_w", [P, W], BF16)
        M["iota_f"] = sb("iota_f", [P, W], F32)
        M["zeros"] = sb("zeros", [P, 512], BF16)
        M["ones"] = sb("ones", [P, P], F32)
        M["deg"] = sb("deg", [P, 4, NT], F32)
        M["wrel"] = sb("wrel", [P, T // (4 * G) - 1, F], F32)
        M["stats"] = sb("stats", [P, 2, NT], F32)
        M["start_row"] = sb("start_row", [P, CELLS], F32)
        M["hT"] = sb("hT", [P, NT, P], F32)
        M["vec"] = sb("vec", [P, len(VECS), F], F32)
        M["prelu"] = sb("prelu", [P, 1], F32)

        D = {}
        D["records"] = dram("records", [P * T, NR], F32)
        D["base"] = dram("base", [KS, CELLS], F32)
        D["starts"] = dram("starts", [CELLS], F32)
        D["tables"] = dram("tables", [3, NTAB * P], I32)
        D["nodes0"] = dram("nodes0", [NT * P, F], F32)
        D["nodes1"] = dram("nodes1", [NT * P * R, F], F32)
        D["count"] = dram("count", [CELLS + 1, P, W], F32)
        D["adj2"] = dram("adj2", [CELLS + 1, P, W], F32)
        D["rows"] = dram("rows", [4 * NT, P], F32)

        with ExitStack() as edges:
            M["edge"] = sb("edge", [EP, EC, NF], F32, edges)
            prepare(nc, A, M, D, edges, sem)
            sort_edges(nc, M, D, sem)
        with ExitStack() as passes:
            M["sorted"] = sb("sorted", [P, T, NR], F32, passes)
            M["cell_of"] = sb("cell_of", [1, T], I32, passes)
            M["offset_of"] = sb("offset_of", [1, T], I32, passes)
            M["nodes"] = sb("nodes", [P, NT, F], F32, passes)
            M["dinv"] = sb("dinv", [P, NT], F32, passes)
            chunk_tables(nc, A, M, D, sem)
            edge_pass(nc, A, M, D, sem, 0)
            relation_tables(nc, M, D, sem)
            edge_pass(nc, A, M, D, sem, 1)
        layer2(nc, A, M, D, sem)
        gcn(nc, A, M, D, sem)
        gat(nc, A, M, D, out, sem)


def prepare(nc, A, M, D, outer, sem):
    with ExitStack() as ctx:
        sb = lambda name, shape, dt: ctx.enter_context(nc.sbuf_tensor(name, shape, dt))
        ps = lambda name, shape, dt: ctx.enter_context(nc.psum_tensor(name, shape, dt))
        edge, x, h = M["edge"], M["x"], M["h"]
        M["iota_cell"] = outer.enter_context(nc.sbuf_tensor("iota_cell", [P, CW], F16))
        M["tri"] = outer.enter_context(nc.sbuf_tensor("tri", [P, P], BF16))
        M["rest"] = outer.enter_context(nc.sbuf_tensor("rest", [P, P], BF16))
        M["base_row"] = outer.enter_context(nc.sbuf_tensor("base_row", [1, KS, CW], F32))
        M["blank"] = outer.enter_context(nc.sbuf_tensor("blank", [P, T, NR], F32))
        src, dst, rel = (sb(n, [EP, EC], I32) for n in ("src_i", "dst_i", "rel_i"))
        w0, w1 = sb("w_raw", [EP, EC], F32), sb("w_rel", [EP, EC], F32)
        ti, tf = sb("t_i", [EP, EC], I32), sb("t_f", [EP, EC], F32)
        sbf, dbf = sb("src_tile", [EP, EC], F32), sb("dst_window", [EP, EC], F32)
        wb = sb("w_bf", [EP, EC], BF16)
        iota_i = sb("iota_i", [P, CW], I32)
        trif = sb("trif", [NT, NT], F32)
        xc, sq = sb("xc", [P, NT, F], F32), sb("sq", [P, NT, F], F32)
        ohs, ohd = sb("hist_src", [EP, 2, G, NT], BF16), sb("hist_dst", [EP, 2, G, NW], BF16)
        hist = sb("hist", [NT, KS, NW], F32)
        tot, cum, cum2 = (sb(n, [NT, NW], F32) for n in ("tot", "cum", "cum2"))
        toti = sb("tot_i", [NT, NW], I32)
        acc = [ps(f"hist_ps{k}", [NT, NW], F32) for k in range(KS)]
        row_ps = ps("row_ps", [NT, 1], F32)

        loaded, x_cleared, x_in = sem("loaded"), sem("x_cleared"), sem("x_in")
        vec_in = sem("vec_in")
        made, sig_done, dve = sem("constants_made"), sem("sig_done"), sem("prep_dve")
        hist_ready, hist_used, row_ready, row_done = sem("hist_ready"), sem("hist_used"), sem("row_ready"), sem("row_done")
        starts_ready, starts_out, starts_in, blank_ready, blank_out = (
            sem(n) for n in ("starts_ready", "starts_out", "starts_in", "blank_ready", "blank_out"))
        var_ready, std_ready = sem("var_ready0"), sem("std_ready0")
        block = ctx.enter_context(nc.Block())

        @block.sync
        def _(sp):
            for t, n in ((src, "src"), (dst, "dst"), (rel, "edge_type_32"), (w0, "edge_weight")):
                sp.dma_start(t[:, :], A[n].rearrange("(p j) -> p j", p=EP)).then_inc(loaded, 16)
            sp.dma_start(w1[:, :], A["edge_weight1"].rearrange("(p j) o -> p (j o)", p=EP)).then_inc(loaded, 16)
            sp.wait_ge(x_cleared, 1)
            sp.dma_start(x[:, 0:NT - 1, :], A["x"][0:(NT - 1) * P, :].rearrange("(t p) f -> p t f", p=P)).then_inc(x_in, 16)
            sp.dma_start(x[0:TAIL, NT - 1, :], A["x"][(NT - 1) * P:N, :]).then_inc(x_in, 16)
            for n, name in enumerate(VECS):
                sp.dma_start(M["vec"][:, n, :], A[name].partition_broadcast(P)).then_inc(vec_in, 16)
            sp.dma_start(M["prelu"][:, :], A["L2_gnn_prelu_a"].partition_broadcast(P)).then_inc(vec_in, 16)
            sp.wait_ge(vec_in, 16 * (len(VECS) + 1))
            sp.wait_ge(blank_ready, 2)
            sp.dma_start(D["records"].rearrange("(p c) f -> p (c f)", p=P), M["blank"][:, :, :].rearrange("p c f -> p (c f)")).then_inc(blank_out, 16)
            sp.wait_ge(starts_ready, 2)
            sp.dma_start(D["base"].rearrange("k (s d) -> s k d", d=NW), hist[:, :, :]).then_inc(starts_out, 16)
            sp.dma_start(D["starts"].rearrange("(s d) -> s d", d=NW), cum2[:, :]).then_inc(starts_out, 16)
            sp.wait_ge(starts_out, 32)
            sp.dma_start(M["base_row"][:, :, 0:CELLS], D["base"].rearrange("(o k) c -> o k c", o=1)).then_inc(starts_in, 16)
            sp.dma_start(M["start_row"][:, :], D["starts"].partition_broadcast(P)).then_inc(starts_in, 16)
            sp.wait_ge(starts_in, 32)
            sp.wait_ge(blank_out, 16)

        @block.gpsimd
        def _(pool):
            nc.gpsimd.iota(iota_i[:, :], [[1, CW]], base=0, channel_multiplier=0).then_inc(made, 1)
            nc.gpsimd.memset(M["ident"][:, :], 0.0).then_inc(made, 1)
            nc.gpsimd.memset(M["ones"][:, :], 1.0).then_inc(made, 1)
            nc.gpsimd.memset(M["tri"][:, :], 1.0).then_inc(made, 1)
            nc.gpsimd.memset(M["rest"][:, :], 1.0).then_inc(made, 1)
            nc.gpsimd.memset(M["zeros"][:, :], 0.0).then_inc(made, 1)
            pool.wait_ge(made, 6)
            nc.gpsimd.affine_select(out=M["ident"][:, :], in_=M["ident"][:, :], compare_op=ALU.not_equal, fill=1.0,
                                    base=0, pattern=[[-1, P]], channel_multiplier=1).then_inc(made, 1)
            nc.gpsimd.affine_select(out=M["tri"][:, :], in_=M["tri"][:, :], compare_op=ALU.is_gt, fill=0.0,
                                    base=0, pattern=[[1, P]], channel_multiplier=-1).then_inc(made, 1)
            nc.gpsimd.affine_select(out=M["rest"][:, :], in_=M["rest"][:, :], compare_op=ALU.is_ge, fill=0.0,
                                    base=0, pattern=[[-1, P]], channel_multiplier=1).then_inc(made, 1)
            nc.gpsimd.memset(M["blank"][:, :, :], 0.0).then_inc(blank_ready, 1)
            pool.wait_ge(blank_ready, 1)
            nc.gpsimd.memset(M["blank"][:, :, S_LOC:S_LOC + 1], -1.0).then_inc(blank_ready, 1)

        @block.scalar
        def _(act):
            act.wait_ge(loaded, 80)
            nc.scalar.activation(edge[:, :, W_SIG], w0[:, :], ACT.Sigmoid).then_inc(sig_done, 1)
            nc.scalar.activation(edge[:, :, W_RAW], w0[:, :], ACT.Copy).then_inc(sig_done, 1)
            nc.scalar.activation(edge[:, :, W_REL], w1[:, :], ACT.Copy).then_inc(sig_done, 1)
            nc.scalar.activation(edge[:, :, SRC], src[:, :], ACT.Copy).then_inc(sig_done, 1)
            nc.scalar.activation(edge[:, :, DST], dst[:, :], ACT.Copy).then_inc(sig_done, 1)
            root_of_variance(nc, act, var_ready, std_ready, M["stats"])

        @block.vector
        def _(v):
            link = linker(v, dve)
            nc.vector.memset(x[:, NT - 1, :], 0.0).then_inc(x_cleared, 1)
            link(nc.vector.memset(M["base_row"][:, :, CELLS:CW], 0.0))
            v.wait_ge(made, 9)
            link(nc.vector.tensor_copy(M["iota_cell"][:, :], iota_i[:, :]))
            link(nc.vector.tensor_copy(M["iota_w"][:, :], iota_i[:, 0:W]))
            link(nc.vector.tensor_copy(M["iota_f"][:, :], iota_i[:, 0:W]))
            link(nc.vector.tensor_copy(M["identb"][:, :], M["ident"][:, :]))
            link(nc.vector.tensor_copy(trif[:, :], M["tri"][0:NT, 0:NT]))
            v.wait_ge(loaded, 80)
            link(nc.vector.tensor_scalar(ti[:, :], src[:, :], 7, None, ALU.arith_shift_right))
            link(nc.vector.tensor_copy(sbf[:, :], ti[:, :]))
            link(nc.vector.tensor_scalar(ti[:, :], dst[:, :], 8, None, ALU.arith_shift_right))
            link(nc.vector.tensor_copy(dbf[:, :], ti[:, :]))
            link(nc.vector.scalar_tensor_tensor(edge[:, :, CELL], sbf[:, :], float(NW), dbf[:, :], ALU.mult, ALU.add))
            iota3 = M["iota_w"][0:EP, :].unsqueeze(1)
            with v.Fori(0, EC // (2 * G)) as i:
                for b in range(2):
                    col = i * (2 * G) + b * G
                    v.wait_ge(hist_used, i * 2 + (b + 1))
                    nc.vector.tensor_tensor(ohs[:, b, :, :], bcast(iota3[:, :, 0:NT], [EP, G, NT]),
                                            bcast(sbf[:, bass.ds(col, G)].unsqueeze(2), [EP, G, NT]),
                                            ALU.is_equal).then_inc(hist_ready, 1)
                    nc.vector.tensor_tensor(ohd[:, b, :, :], bcast(iota3[:, :, 0:NW], [EP, G, NW]),
                                            bcast(dbf[:, bass.ds(col, G)].unsqueeze(2), [EP, G, NW]),
                                            ALU.is_equal).then_inc(hist_ready, 1)
            v.wait_ge(hist_used, 2 + EC // G)
            for k in range(KS):
                link(nc.vector.tensor_copy(hist[:, k, :], acc[k][:, :]))
            link(nc.vector.tensor_tensor(tot[:, :], hist[:, 0, :], hist[:, 1, :], ALU.add))
            link(nc.vector.tensor_tensor(tot[:, :], tot[:, :], hist[:, 2, :], ALU.add))
            link(nc.vector.tensor_tensor(tot[:, :], tot[:, :], hist[:, 3, :], ALU.add))
            link(nc.vector.tensor_scalar(toti[:, :], tot[:, :], float(P - 1), None, ALU.add))
            link(nc.vector.tensor_scalar(toti[:, :], toti[:, :], 7, None, ALU.arith_shift_right))
            link(nc.vector.tensor_scalar(tot[:, :], toti[:, :], 1.0, None, ALU.max))
            a, b, step = cum, cum2, 1
            link(nc.vector.tensor_copy(a[:, :], tot[:, :]))
            while step < NW:
                link(nc.vector.tensor_copy(b[:, 0:step], a[:, 0:step]))
                link(nc.vector.tensor_tensor(b[:, step:NW], a[:, step:NW], a[:, 0:NW - step], ALU.add))
                a, b, step = b, a, 2 * step
            assert a is cum
            nc.vector.tensor_copy(toti[:, 0:1], toti[:, 0:1]).then_inc(row_ready, 1)
            v.wait_ge(row_done, 1)
            link(nc.vector.tensor_tensor(cum2[:, :], cum[:, :], tot[:, :], ALU.subtract))
            link(nc.vector.tensor_scalar(cum2[:, :], cum2[:, :], row_ps[:, 0:1], None, ALU.add))
            for k in range(1, KS - 1):
                link(nc.vector.tensor_tensor(hist[:, k, :], hist[:, k, :], hist[:, k - 1, :], ALU.add))
            for k in range(KS - 1, 0, -1):
                link(nc.vector.scalar_tensor_tensor(hist[:, k, :], cum2[:, :], float(P), hist[:, k - 1, :], ALU.mult, ALU.add))
            link(nc.vector.tensor_scalar(hist[:, 0, :], cum2[:, :], float(P), None, ALU.mult))
            nc.vector.tensor_copy(toti[:, 0:1], toti[:, 0:1]).then_inc(starts_ready, 2)
            link(nc.vector.tensor_scalar(ti[:, :], src[:, :], P - 1, None, ALU.bitwise_and))
            link(nc.vector.tensor_copy(edge[:, :, S_LOC], ti[:, :]))
            link(nc.vector.tensor_scalar(ti[:, :], dst[:, :], W - 1, None, ALU.bitwise_and))
            link(nc.vector.tensor_copy(edge[:, :, D_LOC], ti[:, :]))
            link(nc.vector.tensor_scalar(ti[:, :], dst[:, :], P - 1, None, ALU.bitwise_and))
            link(nc.vector.tensor_copy(edge[:, :, D_LO], ti[:, :]))
            link(nc.vector.tensor_scalar(ti[:, :], dst[:, :], 7, None, ALU.arith_shift_right))
            link(nc.vector.tensor_copy(edge[:, :, D_HI], ti[:, :]))
            link(nc.vector.scalar_tensor_tensor(edge[:, :, SRC_REL], src[:, :], float(R), rel[:, :], ALU.mult, ALU.add))
            v.wait_ge(sig_done, 5)
            link(nc.vector.tensor_copy(tf[:, :], edge[:, :, W_SIG]))
            for f in (W_A, W_B, W_C):
                link(nc.vector.tensor_copy(wb[:, :], tf[:, :]))
                link(nc.vector.tensor_copy(edge[:, :, f], wb[:, :]))
                link(nc.vector.tensor_tensor(tf[:, :], tf[:, :], edge[:, :, f], ALU.subtract))
            v.wait_ge(x_in, 32)
            layer_norm(nc, v, link, var_ready, std_ready, h[:, :, :], x[:, :, :], xc[:, :, :], sq[:, :, :], M["stats"])

        @block.tensor
        def _(pe):
            pe.wait_ge(made, 9)
            for k in range(KS):
                last = nc.tensor.matmul(acc[k][:, :], M["zeros"][:, 0:NT], M["zeros"][:, 0:NW], start=True, stop=True)
            last.then_inc(hist_used, 2)
            with pe.Fori(0, EC // (2 * G)) as i:
                for b in range(2):
                    pe.wait_ge(hist_ready, i * 4 + (2 * b + 2))
                    for k in range(G):
                        last = nc.tensor.matmul(acc[k % KS][:, :], ohs[:, b, k, :], ohd[:, b, k, :], start=False, stop=True,
                                                skip_group_check=True)
                    last.then_inc(hist_used, 1)
            pe.wait_ge(row_ready, 1)
            nc.tensor.matmul(row_ps[:, :], trif[:, :], cum[:, NW - 1:NW], start=True, stop=True).then_inc(row_done, 1)


def sort_edges(nc, M, D, sem):
    with ExitStack() as ctx:
        sb = lambda name, shape, dt: ctx.enter_context(nc.sbuf_tensor(name, shape, dt))
        ps = lambda name, shape, dt: ctx.enter_context(nc.psum_tensor(name, shape, dt))
        edge = M["edge"]
        NB = 4
        NG = 4
        LOOPS = EC // (NB * G)
        stage = sb("stage", [EP, NB, G, NF], F32)
        oh = sb("oh_cell", [EP, NG, KS, CW], BF16)
        junk = sb("junk", [EP, KS, CW], BF16)
        lin, lin_i = sb("lin", [EP, 2, G], F32), sb("lin_i", [EP, 2, G], I32)
        lane, chunk = sb("lane", [EP, 2, G], I32), sb("chunk", [EP, 2, G], I32)
        pos = [sb(f"pos{b}", [EP, G], I32) for b in range(NB)]
        ohl = sb("oh_dlow", [EP, 2, G, P], BF16)
        ohw = sb("oh_dhigh", [EP, 2, G, 4, NT], BF16)
        acc = [ps(f"rank_ps{k}", [EP, CW], F32) for k in range(KS)]
        deg = ps("deg_ps", [P, 4, NT], F32)
        stage_ready, oh_ready, tri_done, sel_done = sem("stage_ready"), sem("oh_ready"), sem("tri_done"), sem("sel_done")
        pos_ready, deg_ready, deg_used, dve = sem("pos_ready"), sem("deg_ready"), sem("deg_used"), sem("sort_dve")
        sent = [sem(f"sent{b}") for b in range(NB)]
        fin = sem("deg_out")
        block = ctx.enter_context(nc.Block())

        @block.scalar
        def _(act):
            def stage_batch(i, b):
                nc.scalar.activation(stage[:, b, :, :], edge[:, bass.ds(i * (NB * G) + b * G, G), :],
                                     ACT.Copy).then_inc(stage_ready, 1)

            for b in range(NB):
                stage_batch(0, b)
            with act.Fori(1, LOOPS) as i:
                for b in range(NB):
                    act.wait_ge(sent[b], i * (16 * G))
                    stage_batch(i, b)

        @block.gpsimd
        def _(pool):
            with pool.Fori(0, LOOPS) as i:
                for b in range(NB):
                    pool.wait_ge(pos_ready, i * NB + (b + 1))
                    pool.sem_inc(M["seen"], 1)
                    for k in range(G):
                        nc.gpsimd.indirect_dma_start(D["records"][:, :],
                                                     bass.IndirectOffsetOnAxis(ap=pos[b][:, k:k + 1], axis=0),
                                                     stage[:, b, k, 0:NR], None).then_inc(sent[b], 16)
            for b in range(NB):
                pool.wait_ge(sent[b], 16 * G * LOOPS)

        @block.vector
        def _(v):
            def one_hots(b, g):
                q = 2 * b + g
                for k in range(KS):
                    last = nc.vector.tensor_scalar(oh[:, q % NG, k, :], M["iota_cell"][0:EP, :],
                                                   stage[:, b % NB, g * KS + k, CELL:CELL + 1], None, ALU.is_equal)
                last.then_inc(oh_ready, 1)

            def low_one_hots(b):
                for k in range(G):
                    nc.vector.tensor_scalar(ohl[:, b % 2, k, :], M["iota_w"][0:EP, 0:P], stage[:, b % NB, k, D_LO:D_LO + 1],
                                            None, ALU.is_equal)

            def high_one_hots(b):
                nc.vector.tensor_tensor(ohw[:, b % 2, :, 0, :], bcast(M["iota_w"][0:EP, 0:NT].unsqueeze(1), [EP, G, NT]),
                                        bcast(stage[:, b % NB, :, D_HI:D_HI + 1], [EP, G, NT]), ALU.is_equal).then_inc(dve, 1)

            def weigh(b):
                for s in range(3):
                    last = nc.vector.tensor_tensor(ohw[:, b % 2, :, 1 + s, :], ohw[:, b % 2, :, 0, :],
                                                   bcast(stage[:, b % NB, :, W_A + s:W_A + s + 1], [EP, G, NT]), ALU.mult)
                last.then_inc(deg_ready, 1)

            def select(i, b, g):
                q = 2 * b + g
                v.wait_ge(tri_done, i * (2 * NB) + (q + 1))
                for k in range(KS):
                    last = nc.vector.tensor_tensor_reduce(
                        out=junk[:, k, :], in0=oh[:, q % NG, k, :], in1=acc[k][:, :], scale=1.0, scalar=0.0,
                        op0=ALU.mult, op1=ALU.add, accum_out=lin[:, b % 2, g * KS + k:g * KS + k + 1])
                last.then_inc(sel_done, 1)

            def body(i, last):
                for b in range(NB):
                    ahead = not (last and b == NB - 1)
                    p, steps = b % 2, 5 if ahead else 4
                    done = i * (5 * NB) + (5 * b + 1)
                    select(i, b, 0)
                    if ahead:
                        v.wait_ge(stage_ready, i * NB + (b + 2))
                        one_hots(b + 1, 0)
                        v.wait_ge(deg_used, i * NB + (b + 2))
                        high_one_hots(b + 1)
                        low_one_hots(b + 1)
                    select(i, b, 1)
                    v.wait_ge(sel_done, i * (2 * NB) + (2 * b + 3))
                    nc.vector.tensor_copy(lin_i[:, p, :], lin[:, p, :]).then_inc(dve, 1)
                    v.wait_ge(dve, done + steps - 3)
                    nc.vector.tensor_scalar(lane[:, p, :], lin_i[:, p, :], P - 1, None, ALU.bitwise_and).then_inc(dve, 1)
                    nc.vector.tensor_scalar(chunk[:, p, :], lin_i[:, p, :], 7, None, ALU.arith_shift_right).then_inc(dve, 1)
                    if ahead:
                        one_hots(b + 1, 1)
                    v.wait_ge(dve, done + steps - 1)
                    nc.vector.scalar_tensor_tensor(pos[b][:, :], lane[:, p, :], float(T), chunk[:, p, :],
                                                   ALU.mult, ALU.add).then_inc(dve, 1)
                    if ahead:
                        weigh(b + 1)
                    v.wait_ge(dve, done + steps)
                    nc.vector.tensor_copy(lane[:, p, 0:1], chunk[:, p, 0:1]).then_inc(pos_ready, 1)

            nc.vector.memset(oh[:, NG - 1, :, :], 0.0).then_inc(sel_done, 1)
            v.wait_ge(stage_ready, 1)
            v.wait_ge(deg_used, 2)
            high_one_hots(0)
            for g in range(2):
                one_hots(0, g)
            low_one_hots(0)
            v.wait_ge(dve, 1)
            weigh(0)
            with v.Fori(0, LOOPS - 1) as i:
                body(i, False)
            body(LOOPS - 1, True)
            v.wait_ge(deg_used, 2 + EC // G)
            nc.vector.tensor_copy(M["deg"][:, :, :], deg[:, :, :]).then_inc(fin, 1)
            v.wait_ge(fin, 1)

        @block.tensor
        def _(pe):
            for k in range(KS):
                nc.tensor.matmul(acc[k][:, :], M["ones"][0:1, 0:EP], M["base_row"][0:1, k, :], start=True, stop=True)
            nc.tensor.matmul(deg[:, :, :], M["zeros"][:, 0:P], M["zeros"][:, 0:4 * NT], start=True,
                             stop=True).then_inc(deg_used, 2)
            with pe.Fori(0, LOOPS) as i:
                for q in range(2 * NB):
                    pe.wait_ge(oh_ready, i * (2 * NB) + (q + 1))
                    pe.wait_ge(sel_done, i * (2 * NB) + (q + 1))
                    for k in range(KS):
                        nc.tensor.matmul(acc[k][:, :], M["rest"][0:EP, 0:EP], oh[:, (q - 1) % NG, k, :],
                                         start=False, stop=True, skip_group_check=True)
                        last = nc.tensor.matmul(acc[k][:, :], M["tri"][0:EP, 0:EP], oh[:, q % NG, k, :],
                                                start=False, stop=True, skip_group_check=True)
                    last.then_inc(tri_done, 1)
                    if q % 2:
                        b = q // 2
                        pe.wait_ge(deg_ready, i * NB + (b + 1))
                        for k in range(G):
                            last = nc.tensor.matmul(deg[:, :, :], ohl[:, b % 2, k, :], ohw[:, b % 2, k, :, :],
                                                    start=False, stop=True, skip_group_check=True)
                        last.then_inc(deg_used, 1)


def spaces(nc, ctx, phase):
    def sb(name, shape, dt):
        return ctx.enter_context(nc.sbuf_tensor(f"{phase}_{name}", shape, dt))

    def ps(name, shape, dt):
        return ctx.enter_context(nc.psum_tensor(f"{phase}_{name}", shape, dt))
    return sb, ps


TB = 4
NTB = -(-NT // TB)


def transposes(nc, pe, h, ident, banks, done, copied):
    for m in range(NTB):
        if m >= 2:
            pe.wait_ge(copied, m - 1)
        for t in range(TB * m, min(TB * m + TB, NT)):
            last = nc.tensor.transpose(banks[m % 2][:, t % TB, :], h[:, t, :], ident)
        last.then_inc(done, 1)


def transposed_out(nc, act, hT, banks, done, copied):
    for m in range(NTB):
        n = min(TB, NT - TB * m)
        act.wait_ge(done, m + 1)
        nc.scalar.activation(hT[:, TB * m:TB * m + n, :], banks[m % 2][:, 0:n, :], ACT.Copy).then_inc(copied, 1)


def products(nc, pe, hT, weights, width, banks, done, taken):
    for t in range(NT):
        if t >= 2:
            pe.wait_ge(taken, t - 1)
        nc.tensor.matmul(banks[t % 2][:, 0:width], hT[:, t, :], weights, start=True, stop=True).then_inc(done, 1)


def chunk_tables(nc, A, M, D, sem):
    with ExitStack() as ctx:
        sb, ps = spaces(nc, ctx, "ct")
        c_i, c_f = sb("c_i", [P, 3, NTAB], I32), sb("c_f", [P, 3, NTAB], F32)
        cmp = sb("cmp", [P, NTAB, CELLS], BF16)
        cell, tile_of = sb("cell", [P, 3, NTAB], F32), sb("tile_of", [P, NTAB], F32)
        val, tab = sb("val", [P, NTAB], F32), sb("tab", [P, 3, NTAB], I32)
        same_i = sb("same_i", [P, T], I32)
        wt, wT, u = sb("w_sn", [P, F], F32), sb("w_snT", [P, F], F32), sb("u", [P, 1], F32)
        v0, sq2, sg = sb("v0", [P, 2], F32), sb("sq2", [P, 2], F32), sb("sg", [P, 2], F32)
        tps = [ps(f"tps{n}", [P, TB, P], F32) for n in range(2)]
        pps = [ps(f"pps{n}", [P, F], F32) for n in range(2)]
        small = ps("small", [P, 8], F32)
        wT_ps = ps("wT_ps", [P, F], F32)
        iota_done, rec_in, w_in, u_in = (sem(f"ct_{n}") for n in ("iota_done", "rec_in", "w_in", "u_in"))
        tab_ready, tab_out, tab_in, dve, root_in, root_out = (
            sem(f"ct_{n}") for n in ("tab_ready", "tab_out", "tab_in", "dve", "root_in", "root_out"))
        tr_done, tr_copied, pr_done, pr_taken, nodes_out, pe_step, dve_step = (
            sem(f"ct_{n}") for n in ("tr_done", "tr_copied", "pr_done", "pr_taken", "nodes_out", "pe_step", "dve_step"))
        block = ctx.enter_context(nc.Block())

        @block.sync
        def _(sp):
            sp.dma_start(wt[:, :], A["L0_gnn_weight"][:, :]).then_inc(w_in, 16)
            sp.dma_start(u[:, :], A["L0_gnn_u"].rearrange("(p o) -> p o", o=1)).then_inc(w_in, 16)
            sp.dma_start(M["sorted"][:, :, :].rearrange("p c f -> p (c f)"),
                         D["records"].rearrange("(p c) f -> p (c f)", p=P)).then_inc(rec_in, 16)
            sp.wait_ge(tab_ready, 1)
            for k in range(3):
                sp.dma_start(D["tables"][k].rearrange("(i p) -> p i", p=P), tab[:, k, :]).then_inc(tab_out, 16)
            sp.wait_ge(tab_out, 48)
            sp.dma_start(M["cell_of"][:, :], D["tables"][0:1, 0:T]).then_inc(tab_in, 16)
            sp.dma_start(M["offset_of"][:, :], D["tables"][1:2, 0:T]).then_inc(tab_in, 16)
            sp.dma_start(same_i[:, :], D["tables"][2, 0:T].partition_broadcast(P)).then_inc(tab_in, 16)
            sp.wait_ge(pr_taken, NT)
            sp.dma_start(D["nodes0"].rearrange("(t p) f -> p t f", p=P), M["nodes"][:, :, :]).then_inc(nodes_out, 16)
            sp.wait_ge(nodes_out, 16)
            sp.wait_ge(rec_in, 16)

        @block.gpsimd
        def _(pool):
            nc.gpsimd.iota(c_i[:, :, :], [[1, 3], [P, NTAB]], base=-1, channel_multiplier=1).then_inc(iota_done, 1)

        @block.scalar
        def _(act):
            act.wait_ge(root_in, 1)
            nc.scalar.activation(M["dinv"][:, :], M["dinv"][:, :], ACT.Sqrt).then_inc(root_out, 1)
            transposed_out(nc, act, M["hT"], tps, tr_done, tr_copied)
            for n in range(2):
                act.wait_ge(root_in, n + 2)
                nc.scalar.activation(sg[:, n:n + 1], small[:, 4 + n:5 + n], ACT.Sqrt).then_inc(root_out, 1)

        @block.vector
        def _(v):
            link = linker(v, dve)
            link(nc.vector.tensor_tensor(M["dinv"][:, :], M["deg"][:, 1, :], M["deg"][:, 2, :], ALU.add))
            link(nc.vector.tensor_tensor(M["dinv"][:, :], M["dinv"][:, :], M["deg"][:, 3, :], ALU.add))
            nc.vector.tensor_scalar(M["dinv"][:, :], M["dinv"][:, :], 1.0, None, ALU.add).then_inc(root_in, 1)
            v.wait_ge(root_out, 1)
            link(nc.vector.reciprocal(M["dinv"][:, :], M["dinv"][:, :]))
            v.wait_ge(pe_step, 2)
            link(nc.vector.tensor_copy(wT[:, :], wT_ps[:, :]))
            link(nc.vector.tensor_copy(v0[:, 0:1], small[:, 0:1]))
            link(nc.vector.tensor_tensor(sq2[:, 0:1], v0[:, 0:1], v0[:, 0:1], ALU.mult))
            nc.vector.tensor_copy(sq2[:, 1:2], sq2[:, 0:1]).then_inc(dve_step, 1)
            v.wait_ge(pe_step, 3)
            nc.vector.tensor_copy(val[:, 0:1], v0[:, 0:1]).then_inc(root_in, 1)
            v.wait_ge(root_out, 2)
            link(nc.vector.tensor_scalar(sg[:, 0:1], sg[:, 0:1], 1e-12, None, ALU.add))
            link(nc.vector.reciprocal(sg[:, 0:1], sg[:, 0:1]))
            nc.vector.tensor_tensor(v0[:, 0:1], v0[:, 0:1], sg[:, 0:1], ALU.mult).then_inc(dve_step, 1)
            v.wait_ge(pe_step, 4)
            link(nc.vector.tensor_copy(v0[:, 1:2], small[:, 1:2]))
            link(nc.vector.tensor_tensor(sq2[:, 0:1], v0[:, 1:2], v0[:, 1:2], ALU.mult))
            nc.vector.tensor_copy(sq2[:, 1:2], sq2[:, 0:1]).then_inc(dve_step, 1)
            v.wait_ge(pe_step, 5)
            nc.vector.tensor_copy(val[:, 0:1], v0[:, 0:1]).then_inc(root_in, 1)
            v.wait_ge(root_out, 3)
            link(nc.vector.tensor_scalar(sg[:, 1:2], sg[:, 1:2], 1e-12, None, ALU.add))
            link(nc.vector.tensor_copy(sq2[:, 0:1], small[:, 5:6]))
            link(nc.vector.reciprocal(sq2[:, 0:1], sq2[:, 0:1]))
            link(nc.vector.tensor_tensor(sg[:, 1:2], sg[:, 1:2], sq2[:, 0:1], ALU.mult))
            v.wait_ge(w_in, 32)
            nc.vector.tensor_scalar(wt[:, :], wt[:, :], sg[:, 1:2], None, ALU.mult).then_inc(dve_step, 1)
            v.wait_ge(iota_done, 1)
            link(nc.vector.tensor_copy(c_f[:, :, :], c_i[:, :, :]))
            for k in range(3):
                link(nc.vector.tensor_tensor(cmp[:, :, :], bcast(M["start_row"][:, :].unsqueeze(1), [P, NTAB, CELLS]),
                                             bcast(c_f[:, k, :].unsqueeze(2), [P, NTAB, CELLS]), ALU.is_le))
                link(nc.vector.tensor_reduce(cell[:, k, :], cmp[:, :, :], AX.X, ALU.add))
                if k == 1:
                    link(nc.vector.tensor_reduce(tile_of[:, :], cmp[:, :, :].rearrange("p i (s d) -> p i s d", d=NW)[:, :, :, 0],
                                                 AX.X, ALU.add))
            link(nc.vector.tensor_scalar(cell[:, 1, :], cell[:, 1, :], 1.0, None, ALU.subtract))
            link(nc.vector.scalar_tensor_tensor(val[:, :], cell[:, 1, :], 1.0, cell[:, 2, :], ALU.add, ALU.is_equal))
            link(nc.vector.tensor_scalar(c_f[:, 2, :], c_f[:, 1, :], float(T - 1), None, ALU.not_equal))
            link(nc.vector.tensor_tensor(val[:, :], val[:, :], c_f[:, 2, :], ALU.mult))
            link(nc.vector.tensor_scalar(c_f[:, 0, :], cell[:, 1, :], -1.0, float(CELLS), ALU.mult, ALU.add))
            link(nc.vector.tensor_tensor(val[:, :], val[:, :], c_f[:, 0, :], ALU.mult))
            link(nc.vector.tensor_tensor(tab[:, 0, :], val[:, :], cell[:, 1, :], ALU.add))
            link(nc.vector.scalar_tensor_tensor(val[:, :], tile_of[:, :], -float(NW), cell[:, 1, :], ALU.mult, ALU.add))
            link(nc.vector.tensor_scalar(tab[:, 1, :], val[:, :], float(NW), float(W), ALU.add, ALU.mult))
            link(nc.vector.scalar_tensor_tensor(tab[:, 2, :], cell[:, 1, :], 1.0, cell[:, 0, :], ALU.add, ALU.is_equal))
            nc.vector.tensor_copy(val[:, 0:1], tile_of[:, 0:1]).then_inc(tab_ready, 1)
            for t in range(NT):
                v.wait_ge(pr_done, t + 1)
                nc.vector.tensor_scalar(M["nodes"][:, t, :], pps[t % 2][:, :], M["dinv"][:, t:t + 1], None,
                                        ALU.mult).then_inc(pr_taken, 1)
            v.wait_ge(tab_in, 48)
            v.wait_ge(rec_in, 16)
            link(nc.vector.tensor_copy(M["sorted"][:, :, SAME], same_i[:, :]))

        @block.tensor
        def _(pe):
            pe.wait_ge(w_in, 32)
            nc.tensor.transpose(wT_ps[:, :], wt[:, :], M["ident"][:, :]).then_inc(pe_step, 1)
            nc.tensor.matmul(small[:, 0:1], wt[:, :], u[:, :], start=True, stop=True).then_inc(pe_step, 1)
            transposes(nc, pe, M["h"], M["ident"][:, :], tps, tr_done, tr_copied)
            pe.wait_ge(dve_step, 1)
            nc.tensor.matmul(small[:, 4:5], M["ones"][:, :], sq2[:, 0:1], start=True, stop=True).then_inc(pe_step, 1)
            pe.wait_ge(dve_step, 2)
            nc.tensor.matmul(small[:, 1:2], wT[:, :], v0[:, 0:1], start=True, stop=True).then_inc(pe_step, 1)
            pe.wait_ge(dve_step, 3)
            nc.tensor.matmul(small[:, 5:6], M["ones"][:, :], sq2[:, 0:1], start=True, stop=True).then_inc(pe_step, 1)
            pe.wait_ge(dve_step, 4)
            pe.wait_ge(tr_copied, NTB)
            products(nc, pe, M["hT"], wt[:, :], F, pps, pr_done, pr_taken)


def edge_pass(nc, A, M, D, sem, layer):
    with ExitStack() as ctx:
        sb, ps = spaces(nc, ctx, f"pass{layer}")
        s = lambda name: sem(f"{name}_{layer}")
        table = D["nodes0"] if layer == 0 else D["nodes1"]
        blocks = D["count"] if layer == 0 else D["adj2"]
        index, weight = (SRC, W_SIG) if layer == 0 else (SRC_REL, W_REL)
        NB = 4
        LOOPS = T // (NB * G)
        stage = sb("stage", [P, NB, G, NR], F32)
        idx = [sb(f"idx{b}", [P, G], I32) for b in range(NB)]
        rows = [sb(f"rows{b}", [P, G, F], F32) for b in range(NB)]
        od = sb("one_dst", [P, 2, G, W], F32)
        os = sb("one_src", [P, 2, G, P], F32)
        PAIRS = G // 2
        FREE = 2 + G
        blk = sb("blk", [P, 2 * G, W], F32)
        pair = sb("pair", [P, 2, 2, W], F32)
        if layer == 0:
            assert R <= LOOPS - 1 and 1 + B <= NB * PAIRS
            wbase, wcomp = sb("wbase", [P, B, F], F32), sb("wcomp", [P, (LOOPS - 1) * B], F32)
            comp, wacc = sb("comp", [P, B], F32), sb("wacc", [P, F], F32)
            comp_clear, weights_in, wrel_step = s("comp_clear"), s("weights_in"), s("wrel_step")
        xc, sq = M["hT"], M["nodes"]
        loop_w = sb("loop_w", [P, F], F32)
        sums = ps("sums", [P, 3584], F32)
        blk_ps = ps("blk_ps", [P, 2, W], F32)
        idx_ready, stage_ready, scaled, oh_ready, pe_done, blk_mm, pair_out, blk_taken, blk_free = (
            s(n) for n in ("idx_ready", "stage_ready", "scaled", "oh_ready", "pe_done", "blk_mm", "pair_out", "blk_taken",
                           "blk_free"))
        gathered, written = [s(f"gathered{b}") for b in range(NB)], s("written")
        dve, var_ready, std_ready = (s(n) for n in ("dve", "var_ready", "std_ready"))
        loop_in = s("loop_in") if layer == 1 else None
        block = ctx.enter_context(nc.Block())

        @block.scalar
        def _(act):
            def stage_index(i, b):
                nc.scalar.activation(idx[b % NB][:, :], M["sorted"][:, bass.ds(i * (NB * G) + b * G, G), index],
                                     ACT.Copy).then_inc(idx_ready, 1)

            def stage_fields(i, b):
                nc.scalar.activation(stage[:, b % NB, :, :], M["sorted"][:, bass.ds(i * (NB * G) + b * G, G), :],
                                     ACT.Copy).then_inc(stage_ready, 1)

            def scale(b, k):
                return nc.scalar.activation(rows[b % NB][:, k, :], rows[b % NB][:, k, :], ACT.Copy,
                                            scale=stage[:, b % NB, k, weight:weight + 1])

            def body(i, last):
                for b in range(NB):
                    if not last:
                        stage_index(i, b + NB)
                    for j in range(PAIRS):
                        pairs = i * (NB * PAIRS) + (b * PAIRS + j)
                        act.wait_ge(blk_mm, pairs + 1)
                        act.wait_ge(blk_taken, i * (NB * G) + (b * G + 2 * j + FREE - 2))
                        nc.scalar.activation(pair[:, j % 2, :, :], blk_ps[:, :, :], ACT.Copy).then_inc(pair_out, 1)
                        if not (last and b == NB - 1):
                            if j == 0:
                                act.wait_ge(gathered[(b + 1) % NB], (i + (b + 1) // NB + 1) * (16 * G))
                                act.wait_ge(stage_ready, i * NB + (b + 2))
                            scale(b + 1, 2 * j)
                            scale(b + 1, 2 * j + 1).then_inc(scaled, 1)
                        if j == 1 and not (last and b >= NB - 2):
                            stage_fields(i, b + 2)

            act.sem_inc(pair_out, 1)
            for b in range(NB):
                stage_index(0, b)
            for b in range(2):
                stage_fields(0, b)
            act.wait_ge(gathered[0], 16 * G)
            act.wait_ge(stage_ready, 1)
            for j in range(PAIRS):
                scale(0, 2 * j)
                scale(0, 2 * j + 1).then_inc(scaled, 1)
            with act.Fori(0, LOOPS - 1) as i:
                body(i, False)
            body(LOOPS - 1, True)
            root_of_variance(nc, act, var_ready, std_ready, M["stats"])

        @block.gpsimd
        def _(pool):
            with pool.Fori(0, LOOPS) as i:
                for b in range(NB):
                    pool.wait_ge(idx_ready, i * NB + (b + 1))
                    pool.sem_inc(M["seen"], 1)
                    pool.wait_ge(pe_done, i * NB + (b + 1))
                    pool.sem_inc(M["seen"], 1)
                    for k in range(G):
                        nc.gpsimd.indirect_dma_start(rows[b][:, k, :], None, table[:, :],
                                                     bass.IndirectOffsetOnAxis(ap=idx[b][:, k:k + 1], axis=0)
                                                     ).then_inc(gathered[b], 16)

        @block.sync
        def _(sp):
            if layer == 1:
                sp.dma_start(loop_w[:, :], A["L1_gnn_loop_weight"][:, :]).then_inc(loop_in, 16)
            sp.sem_inc(blk_free, 2)
            if layer == 0:
                sp.wait_ge(comp_clear, 1)
                sp.dma_start(wbase[:, :, :], A["L1_gnn_weight"].rearrange("b d f -> d b f")).then_inc(weights_in, 16)
                sp.dma_start(wcomp[:, 0:R * B], A["L1_gnn_w_comp"].rearrange("r b -> (r b)").partition_broadcast(P)
                             ).then_inc(weights_in, 16)
            with sp.Fori(0, LOOPS) as i:
                for b in range(NB):
                    cells = nc.values_load_multi_w_load_instructions(
                        M["cell_of"][0:1, bass.ds(i * (NB * G) + b * G, G)], engines=[mybir.EngineType.SP],
                        min_val=0, max_val=CELLS)[1]
                    for k in range(G):
                        sp.wait_ge(blk_taken, i * (NB * G) + (b * G + k + 1 + FREE))
                        sp.dma_start(blocks[bass.ds(cells[k], 1), :, :].rearrange("o p w -> p (o w)"),
                                     blk[:, (b % 2) * G + k, :], cond=cells[k] < CELLS).then_inc(written, 16)
                    sp.wait_ge(written, i * (NB * 16 * G) + (b + 1) * (16 * G))
                    sp.sem_inc(blk_free, 1)

        @block.vector
        def _(v):
            def one_hots(b, k):
                f = lambda n: stage[:, b % NB, k, n:n + 1]
                nc.vector.tensor_scalar(od[:, b % 2, k, :], M["iota_f"][:, :], f(D_LOC), None, ALU.is_equal)
                if layer == 0:
                    return nc.vector.tensor_scalar(os[:, b % 2, k, :], M["iota_f"][:, 0:P], f(S_LOC), None, ALU.is_equal)
                return nc.vector.tensor_scalar(os[:, b % 2, k, :], M["iota_f"][:, 0:P], f(S_LOC), f(W_RAW),
                                               ALU.is_equal, ALU.mult)

            def take(i, b, k):
                at = (b % 2) * G + k
                v.wait_ge(blk_taken, i * (NB * G) + (b * G + k + FREE))
                nc.vector.scalar_tensor_tensor(blk[:, at, :], blk[:, (at - 1) % (2 * G), :], stage[:, b, k, SAME:SAME + 1],
                                               pair[:, k // 2 % 2, k % 2, :], ALU.mult, ALU.add).then_inc(blk_taken, 1)

            def relation_weights(i, step):
                v.wait_ge(wrel_step, i * (1 + B) + (step + 1))
                if step == 0:
                    ins = nc.vector.tensor_copy(comp[:, :], wcomp[:, bass.ds(i * B, B)])
                elif step == 1:
                    ins = nc.vector.tensor_scalar(wacc[:, :], wbase[:, 0, :], comp[:, 0:1], None, ALU.mult)
                elif step < B:
                    ins = nc.vector.scalar_tensor_tensor(wacc[:, :], wbase[:, step - 1, :], comp[:, step - 1:step], wacc[:, :],
                                                         ALU.mult, ALU.add)
                else:
                    ins = nc.vector.scalar_tensor_tensor(M["wrel"][:, bass.ds(i, 1), :], wbase[:, B - 1:B, :], comp[:, B - 1:B],
                                                         wacc[:, :].unsqueeze(1), ALU.mult, ALU.add)
                ins.then_inc(wrel_step, 1)

            def body(i, last):
                for b in range(NB):
                    v.wait_ge(blk_free, i * NB + (b + 1))
                    for j in range(PAIRS):
                        v.wait_ge(pair_out, i * (NB * PAIRS) + (b * PAIRS + j + 2))
                        take(i, b, 2 * j)
                        take(i, b, 2 * j + 1)
                        if last and b == NB - 1:
                            continue
                        if j == 0:
                            v.wait_ge(stage_ready, i * NB + (b + 2))
                        one_hots(b + 1, 2 * j)
                        one_hots(b + 1, 2 * j + 1).then_inc(oh_ready, 1)
                        if layer == 0 and not last and b * PAIRS + j < 1 + B:
                            relation_weights(i, b * PAIRS + j)

            nc.vector.memset(blk[:, :, :], 0.0).then_inc(blk_taken, FREE)
            if layer == 0:
                nc.vector.memset(wcomp[:, :], 0.0).then_inc(comp_clear, 1)
                v.sem_inc(wrel_step, 1)
                v.wait_ge(weights_in, 32)
            v.wait_ge(stage_ready, 1)
            for j in range(PAIRS):
                one_hots(0, 2 * j)
                one_hots(0, 2 * j + 1).then_inc(oh_ready, 1)
            with v.Fori(0, LOOPS - 1) as i:
                body(i, False)
            body(LOOPS - 1, True)
            v.wait_ge(pe_done, NB + NB * LOOPS)
            link = linker(v, dve)
            agg = sums[:, 0:NT * F].rearrange("p (t f) -> p t f", f=F)
            full = [P, NT, F]
            x, h = M["x"][:, :, :], M["h"][:, :, :]
            bias = bcast(M["vec"][:, B0 if layer == 0 else B1, :].unsqueeze(1), full)
            if layer == 0:
                link(nc.vector.tensor_tensor(xc[:, :, :], agg, M["nodes"][:, :, :], ALU.add))
                link(nc.vector.tensor_tensor(xc[:, :, :], xc[:, :, :], bcast(M["dinv"][:, :].unsqueeze(2), full), ALU.mult))
                link(nc.vector.tensor_tensor(xc[:, :, :], xc[:, :, :], bias, ALU.add))
                link(nc.vector.tensor_tensor(x, xc[:, :, :], x, ALU.add))
            else:
                link(nc.vector.tensor_tensor(xc[:, :, :], agg, bias, ALU.add))
                link(nc.vector.scalar_tensor_tensor(x, xc[:, :, :], 0.0, x, ALU.max, ALU.add))
            layer_norm(nc, v, link, var_ready, std_ready, h, x, xc[:, :, :], sq[:, :, :], M["stats"])

        @block.tensor
        def _(pe):
            for n in range(7):
                last = nc.tensor.matmul(sums[:, 512 * n:512 * n + 512], M["zeros"][:, 0:P], M["zeros"][:, :],
                                        start=True, stop=True)
            last.then_inc(pe_done, NB)
            if layer == 1:
                pe.wait_ge(loop_in, 16)
                for t in range(NT):
                    nc.tensor.matmul(sums[:, t * F:(t + 1) * F], M["hT"][:, t, :], loop_w[:, :], start=False, stop=True,
                                     skip_group_check=True)
            with pe.Fori(0, LOOPS) as i:
                for b in range(NB):
                    p = b % 2
                    for j in range(PAIRS):
                        pe.wait_ge(pair_out, i * (NB * PAIRS) + (b * PAIRS + j + 1))
                        pe.wait_ge(oh_ready, i * (NB * PAIRS) + (b * PAIRS + j + 1))
                        for k in (2 * j, 2 * j + 1):
                            if layer == 0:
                                ins = nc.tensor.matmul(blk_ps[:, k % 2, :], os[:, p, k, :], od[:, p, k, :],
                                                       start=True, stop=True)
                            else:
                                for half in range(2):
                                    ins = nc.tensor.matmul(blk_ps[:, k % 2, half * P:half * P + P],
                                                           od[:, p, k, half * P:half * P + P], os[:, p, k, :],
                                                           start=True, stop=True)
                        ins.then_inc(blk_mm, 1)
                        offs = nc.values_load_multi_w_load_instructions(
                            M["offset_of"][0:1, bass.ds(i * (NB * G) + b * G + 2 * j, 2)], engines=[mybir.EngineType.PE],
                            min_val=0, max_val=(NW - 1) * W)[1]
                        pe.wait_ge(scaled, i * (NB * PAIRS) + (b * PAIRS + j + 1))
                        for k in (2 * j, 2 * j + 1):
                            for half in range(2):
                                ins = nc.tensor.matmul(sums[:, bass.ds(offs[k % 2] + half * P, P)],
                                                       od[:, p, k, half * P:half * P + P], rows[b][:, k, :],
                                                       start=False, stop=True, skip_group_check=True)
                    ins.then_inc(pe_done, 1)


def relation_tables(nc, M, D, sem):
    with ExitStack() as ctx:
        sb, ps = spaces(nc, ctx, "rt")
        Q = R * F // 512
        y = sb("y", [P, 2, R * F], F32)
        tps = [ps(f"tps{n}", [P, TB, P], F32) for n in range(2)]
        yps = [ps(f"yps{n}", [P, 512], F32) for n in range(6)]
        tr_done, tr_copied, mm, taken_a, taken_v, stored = (
            sem(f"rt_{n}") for n in ("tr_done", "tr_copied", "mm", "taken_a", "taken_v", "stored"))
        wrel = M["wrel"][:, 0:R, :].rearrange("p r f -> p (r f)")
        out_rows = D["nodes1"].rearrange("(t p r) f -> t p (r f)", p=P, r=R)
        block = ctx.enter_context(nc.Block())
        stores = [sem(f"rt_store{b}") for b in range(2)]

        @block.tensor
        def _(pe):
            transposes(nc, pe, M["h"], M["ident"][:, :], tps, tr_done, tr_copied)
            pe.wait_ge(tr_copied, NTB)
            for n in range(NT * Q):
                if n >= 6:
                    pe.wait_ge(taken_v if n % 2 else taken_a, (n - 6) // 2 + 1)
                nc.tensor.matmul(yps[n % 6][:, :], M["hT"][:, n // Q, :], wrel[:, (n % Q) * 512:(n % Q) * 512 + 512],
                                 start=True, stop=True).then_inc(mm, 1)

        def take(eng, copy, parity, taken):
            for t in range(NT):
                if t >= 2:
                    eng.wait_ge(stores[t % 2], 16 * (t // 2))
                for q in range(parity, Q, 2):
                    n = Q * t + q
                    eng.wait_ge(mm, n + 1)
                    copy(y[:, t % 2, q * 512:q * 512 + 512], yps[n % 6][:, :]).then_inc(taken, 1)

        @block.scalar
        def _(act):
            transposed_out(nc, act, M["hT"], tps, tr_done, tr_copied)
            take(act, lambda o, i: nc.scalar.activation(o, i, ACT.Copy), 0, taken_a)

        @block.vector
        def _(v):
            take(v, nc.vector.tensor_copy, 1, taken_v)

        @block.sync
        def _(sp):
            for t in range(NT):
                sp.wait_ge(taken_a, (t + 1) * Q // 2)
                sp.wait_ge(taken_v, (t + 1) * Q // 2)
                sp.dma_start(out_rows[t], y[:, t % 2, :]).then_inc(stores[t % 2], 16)
            for b in range(2):
                sp.wait_ge(stores[b], 16 * ((NT + 1 - b) // 2))


def layer2(nc, A, M, D, sem):
    with ExitStack() as ctx:
        sb, ps = spaces(nc, ctx, "l2")
        s = lambda n: sem(f"l2_{n}")
        w, wT = sb("w2", [P, F], F32), sb("w2T", [P, F], F32)
        tab = sb("tab2", [P, 2 * NW, F], F32)
        adj = [sb(f"adj{b}", [P, NW, W], F32) for b in range(2)]
        agg, xc, sq = (sb(n, [P, NT, F], F32) for n in ("agg2", "xc3", "sq3"))
        tps = [ps(f"tps{n}", [P, TB, P], F32) for n in range(2)]
        pps = [ps(f"pps{n}", [P, F], F32) for n in range(2)]
        aps = [ps(f"aps{n}", [P, F], F32) for n in range(2)]
        wT_ps = ps("wT_ps", [P, F], F32)
        w_in, wT_done, wT_copied, tr_done, tr_copied, pr_done, pr_taken = (
            s(n) for n in ("w_in", "wT_done", "wT_copied", "tr_done", "tr_copied", "pr_done", "pr_taken"))
        in_, summed, taken, dve, var_ready, std_ready = ([s("in0"), s("in1")], s("summed"), s("taken"), s("dve"),
                                                         s("var_ready"), s("std_ready"))
        cells = D["adj2"][0:CELLS].rearrange("(t c) p w -> t p c w", c=NW)
        block = ctx.enter_context(nc.Block())

        @block.sync
        def _(sp):
            sp.dma_start(w[:, :], A["L2_gnn_W"][:, :]).then_inc(w_in, 16)
            for t in range(2):
                sp.dma_start(adj[t][:, :, :], cells[t]).then_inc(in_[t], 16)
            with sp.Fori(0, NT // 2 - 1) as i:
                for b in range(2):
                    sp.wait_ge(summed, i * 2 + (b + 1))
                    sp.dma_start(adj[b][:, :, :],
                                 cells[bass.ds(i * 2 + (b + 2), 1)].rearrange("t p c w -> p (t c) w")).then_inc(in_[b], 16)
            sp.wait_ge(summed, NT - 2)
            sp.dma_start(adj[0][:, :, :], cells[NT - 1]).then_inc(in_[0], 16)
            sp.wait_ge(in_[0], 16 * (NT // 2 + 1))

        @block.scalar
        def _(act):
            act.wait_ge(wT_done, 1)
            nc.scalar.activation(wT[:, :], wT_ps[:, :], ACT.Copy).then_inc(wT_copied, 1)
            transposed_out(nc, act, M["hT"], tps, tr_done, tr_copied)
            root_of_variance(nc, act, var_ready, std_ready, M["stats"])

        @block.vector
        def _(v):
            link = linker(v, dve)
            link(nc.vector.memset(tab[:, NT, :], 0.0))
            for t in range(NT):
                v.wait_ge(pr_done, t + 1)
                nc.vector.tensor_copy(tab[:, t, :], pps[t % 2][:, :]).then_inc(pr_taken, 1)
            with v.Fori(0, NT // 2) as i:
                for b in range(2):
                    v.wait_ge(summed, i * 2 + (b + 1))
                    nc.vector.tensor_copy(agg[:, bass.ds(i * 2 + b, 1), :], aps[b][:, :].unsqueeze(1)).then_inc(taken, 1)
            v.wait_ge(summed, NT)
            link(nc.vector.tensor_copy(agg[:, NT - 1, :], aps[0][:, :]))
            v.wait_ge(taken, NT - 1)
            full = [P, NT, F]
            x, h = M["x"][:, :, :], M["h"][:, :, :]
            link(nc.vector.tensor_tensor(agg[:, :, :], agg[:, :, :], bcast(M["vec"][:, B2, :].unsqueeze(1), full), ALU.add))
            link(nc.vector.tensor_scalar(xc[:, :, :], agg[:, :, :], 0.0, M["prelu"][:, 0:1], ALU.min, ALU.mult))
            link(nc.vector.scalar_tensor_tensor(xc[:, :, :], agg[:, :, :], 0.0, xc[:, :, :], ALU.max, ALU.add))
            link(nc.vector.tensor_tensor(x, x, xc[:, :, :], ALU.add))
            layer_norm(nc, v, link, var_ready, std_ready, h, x, xc[:, :, :], sq[:, :, :], M["stats"])

        @block.tensor
        def _(pe):
            pe.wait_ge(w_in, 16)
            nc.tensor.transpose(wT_ps[:, :], w[:, :], M["ident"][:, :]).then_inc(wT_done, 1)
            transposes(nc, pe, M["h"], M["ident"][:, :], tps, tr_done, tr_copied)
            pe.wait_ge(tr_copied, NTB)
            pe.wait_ge(wT_copied, 1)
            products(nc, pe, M["hT"], wT[:, :], F, pps, pr_done, pr_taken)
            pe.wait_ge(pr_taken, NT)
            pe.wait_ge(dve, 1)

            def tile_sum(b):
                for n in range(2 * NW):
                    last = nc.tensor.matmul(aps[b][:, :], adj[b][:, n // 2, (n % 2) * P:(n % 2) * P + P], tab[:, n, :],
                                            start=(n == 0), stop=(n == 2 * NW - 1))
                last.then_inc(summed, 1)

            for b in range(2):
                pe.wait_ge(in_[b], 16)
                tile_sum(b)
            with pe.Fori(1, NT // 2) as i:
                for b in range(2):
                    pe.wait_ge(in_[b], i * 16 + 16)
                    pe.wait_ge(taken, i * 2 + (b - 1))
                    tile_sum(b)
            pe.wait_ge(in_[0], 16 * (NT // 2 + 1))
            pe.wait_ge(taken, NT - 2)
            tile_sum(0)


def gcn(nc, A, M, D, sem):
    with ExitStack() as ctx:
        sb, ps = spaces(nc, ctx, "gcn")
        s = lambda n: sem(f"gcn_{n}")
        w = sb("w3", [P, F], F32)
        tab = sb("tab3", [P, NT, F], F32)
        dinv = sb("dinv3", [P, NT], F32)
        cnt = [sb(f"cnt{b}", [P, NT, W], F32) for b in range(2)]
        agg, xc, sq = sb("agg3", [P, 2 * NW, F], F32), sb("xc4", [P, NT, F], F32), sb("sq4", [P, NT, F], F32)
        tps = [ps(f"tps{n}", [P, TB, P], F32) for n in range(2)]
        pps = [ps(f"pps{n}", [P, F], F32) for n in range(2)]
        aps = [[ps(f"aps{n}{h}", [P, F], F32) for h in range(2)] for n in range(2)]
        w_in, tr_done, tr_copied, pr_done, pr_taken, root_in, root_out = (
            s(n) for n in ("w_in", "tr_done", "tr_copied", "pr_done", "pr_taken", "root_in", "root_out"))
        in_, summed, taken, dve, var_ready, std_ready, sig = ([s("in0"), s("in1")], s("summed"), s("taken"), s("dve"),
                                                              s("var_ready"), s("std_ready"), s("sig"))
        cells = D["count"][0:CELLS].rearrange("(t c) p w -> c p t w", c=NW)
        block = ctx.enter_context(nc.Block())

        @block.sync
        def _(sp):
            sp.dma_start(w[:, :], A["L3_gnn_gcn_w"][:, :]).then_inc(w_in, 16)
            for g in range(2):
                sp.dma_start(cnt[g][:, :, :], cells[g]).then_inc(in_[g], 16)
            with sp.Fori(0, NW // 2 - 1) as i:
                for b in range(2):
                    sp.wait_ge(summed, i * 2 + (b + 1))
                    sp.dma_start(cnt[b][:, :, :], cells[bass.ds(i * 2 + (b + 2), 1)].rearrange("c p t w -> p (c t) w")).then_inc(in_[b], 16)
            sp.wait_ge(summed, NW - 2)
            sp.dma_start(cnt[0][:, :, :], cells[NW - 1]).then_inc(in_[0], 16)
            sp.wait_ge(in_[0], 16 * (NW // 2 + 1))

        @block.scalar
        def _(act):
            act.wait_ge(root_in, 1)
            nc.scalar.activation(dinv[:, :], dinv[:, :], ACT.Sqrt).then_inc(root_out, 1)
            transposed_out(nc, act, M["hT"], tps, tr_done, tr_copied)
            root_of_variance(nc, act, var_ready, std_ready, M["stats"])
            act.wait_ge(sig, 1)
            nc.scalar.activation(sq[:, :, :], xc[:, :, :], ACT.Sigmoid).then_inc(sig, 1)

        @block.vector
        def _(v):
            link = linker(v, dve)
            nc.vector.tensor_scalar(dinv[:, :], M["deg"][:, 0, :], 1.0, None, ALU.add).then_inc(root_in, 1)
            v.wait_ge(root_out, 1)
            link(nc.vector.reciprocal(dinv[:, :], dinv[:, :]))
            for t in range(NT):
                v.wait_ge(pr_done, t + 1)
                nc.vector.tensor_scalar(tab[:, t, :], pps[t % 2][:, :], dinv[:, t:t + 1], None, ALU.mult).then_inc(pr_taken, 1)

            with v.Fori(0, NW // 2) as i:
                for b in range(2):
                    v.wait_ge(summed, i * 2 + (b + 1))
                    for h in range(2):
                        nc.vector.tensor_copy(agg[:, bass.ds(i * 4 + (2 * b + h), 1), :], aps[b][h][:, :].unsqueeze(1)).then_inc(taken, 1)
            v.wait_ge(summed, NW)
            link(nc.vector.tensor_copy(agg[:, NT - 1, :], aps[0][0][:, :]))
            v.wait_ge(taken, 2 * (NW - 1))
            full = [P, NT, F]
            g = agg[:, 0:NT, :]
            h = M["h"][:, :, :]
            vec = lambda n: bcast(M["vec"][:, n, :].unsqueeze(1), full)
            link(nc.vector.tensor_tensor(g, g, tab[:, :, :], ALU.add))
            link(nc.vector.tensor_tensor(g, g, bcast(dinv[:, :].unsqueeze(2), full), ALU.mult))
            link(nc.vector.tensor_tensor(g, g, vec(B_GCN), ALU.add))
            layer_norm(nc, v, link, var_ready, std_ready, h, g, xc[:, :, :], sq[:, :, :], M["stats"], relu=False)
            link(nc.vector.tensor_tensor(h, h, vec(GAMMA), ALU.mult))
            nc.vector.tensor_tensor(xc[:, :, :], h, vec(BETA), ALU.add).then_inc(sig, 1)
            v.wait_ge(sig, 2)
            link(nc.vector.tensor_tensor(h, xc[:, :, :], sq[:, :, :], ALU.mult))

        @block.tensor
        def _(pe):
            transposes(nc, pe, M["h"], M["ident"][:, :], tps, tr_done, tr_copied)
            pe.wait_ge(tr_copied, NTB)
            pe.wait_ge(w_in, 16)
            products(nc, pe, M["hT"], w[:, :], F, pps, pr_done, pr_taken)
            pe.wait_ge(pr_taken, NT)

            def window_sum(b):
                for h in range(2):
                    for t in range(NT):
                        last = nc.tensor.matmul(aps[b][h][:, :], cnt[b][:, t, h * P:h * P + P], tab[:, t, :],
                                                start=(t == 0), stop=(t == NT - 1))
                last.then_inc(summed, 1)

            for b in range(2):
                pe.wait_ge(in_[b], 16)
                window_sum(b)
            with pe.Fori(1, NW // 2) as i:
                for b in range(2):
                    pe.wait_ge(in_[b], i * 16 + 16)
                    pe.wait_ge(taken, i * 4 + (2 * b - 2))
                    window_sum(b)
            pe.wait_ge(in_[0], 16 * (NW // 2 + 1))
            pe.wait_ge(taken, 2 * (NW - 2))
            window_sum(0)


def gat(nc, A, M, D, out, sem):
    with ExitStack() as ctx:
        sb, ps = spaces(nc, ctx, "gat")
        s = lambda n: sem(f"gat_{n}")
        H = 2
        AW = H * F + 2 * H
        att = sb("att", [P, 2 * H, F], F32)
        haug = sb("haug", [P, NT, H, F + 1], F32)
        acol = sb("acol", [P, 2 * H, NT], F32)
        acol5 = sb("acol5", [P, NT, H], F32)
        arow_s, arow = sb("arow_s", [H * NT, P], F32), sb("arow", [P, H, NT * P], F32)
        cnt = [sb(f"cnt{b}", [P, NT, W], F32) for b in range(2)]
        pen = sb("pen", [P, NT, W], BF16)
        mx, m, e = sb("mx", [P, 2, H, NTB], F32), sb("m", [P, 2, H], F32), sb("e", [P, 2, H], F32)
        r12 = sb("r12", [P, 2, 2, H], F32)
        diag = sb("diag", [P, 2, 2, H, P], F32)
        t2, z, ex, pm = (sb(n, [P, 2, H, W], F32) for n in ("t2", "z", "ex", "pm"))
        junk = sb("junk", [P, 2 * H, TB * P], BF16)
        w = junk[:, :, :].rearrange("p n c -> p (n c)").bitcast(F32)[:, 0:AW]
        LOAD = 5
        PARTS = NT // LOAD
        OWN_AT, MAX_AT = 3, 5
        CREDIT = 2
        assert NT % 2
        rec = sb("rec", [P, 2, H], F32)
        part, scratch = att[:, 0:2, :], z[:, 0, 0, 0:F]
        tps = [ps(f"tps{n}", [P, 512], F32) for n in range(2)]
        rps = [[ps(f"rps{n}{q}", [P, H, W], F32) for q in range(2)] for n in range(2)]
        aps = [ps(f"aps{n}", [P, 512], F32) for n in range(2)]
        ops = [t[:, 0:H * (F + 1)].rearrange("p (h f) -> p h f", h=H) for t in aps]
        w_in, wv, tr_done, tr_copied, pr_done, pr_taken, at_done, at_copied, row_out, row_in, dve = (
            s(n) for n in ("w_in", "wv", "tr_done", "tr_copied", "pr_done", "pr_taken", "at_done", "at_copied", "row_out",
                           "row_in", "dve"))
        in_, pen_ready, pt_done, pt_taken, diag_ready, rows_mm, group_done = (
            [s("in0"), s("in1")], s("pen_ready"), s("pt_done"), s("pt_taken"), s("diag_ready"), s("rows_mm"),
            s("group_done"))
        t2_done, z_done, ex_done, pm_done, mm_done, chain, self_added = (
            s(n) for n in ("t2_done", "z_done", "ex_done", "pm_done", "mm_done", "chain", "self_added"))
        var_ready, std_ready, sig, o_ready, stored = s("var_ready"), s("std_ready"), s("sig"), s("o_ready"), s("stored")
        acc_g = M["wrel"][:, 0:NT, :]
        cells = D["count"][0:CELLS].rearrange("(t c) p w -> c p t w", c=NW)
        tb16 = [t[:, :].bitcast(BF16).rearrange("p (h c) -> p h c", h=2) for t in tps]
        block = ctx.enter_context(nc.Block())

        @block.sync
        def _(sp):
            sp.dma_start(w[:, 0:H * F], A["L3_gnn_gat_w"][:, :]).then_inc(w_in, 16)
            for n, name in enumerate(("L3_gnn_att_src", "L3_gnn_att_dst")):
                sp.dma_start(att[:, n * H:n * H + H, :].rearrange("p h f -> p (h f)"),
                             A[name].rearrange("h f -> (h f)").partition_broadcast(P)).then_inc(w_in, 16)
            for g in range(2):
                for tiles in (slice(n, n + LOAD) for n in range(0, NT, LOAD)):
                    sp.dma_start(cnt[g][:, tiles, :], cells[g][:, tiles, :]).then_inc(in_[g], 16)
            sp.wait_ge(at_copied, 1)
            sp.dma_start(D["rows"][0:H * NT, :], arow_s[:, :]).then_inc(row_out, 16)
            sp.wait_ge(row_out, 16)
            sp.dma_start(arow[:, :, :].rearrange("p h n -> p (h n)"),
                         D["rows"][0:H * NT, :].rearrange("a n -> (a n)").partition_broadcast(P)).then_inc(row_in, 16)
            def load(g, b, src):
                for part in range(PARTS):
                    tiles = slice(LOAD * part, LOAD * part + LOAD)
                    sp.wait_ge(pm_done, g * NT + (LOAD * part + LOAD + CREDIT))
                    sp.dma_start(cnt[b][:, tiles, :], src[:, tiles, :]).then_inc(in_[b], 16)

            with sp.Fori(0, NW // 2 - 1) as i:
                for b in range(2):
                    load(i * 2 + b, b, cells[bass.ds(i * 2 + (b + 2), 1)].rearrange("c p t w -> p (c t) w"))
            load(NW - 3, 0, cells[NW - 1])
            sp.wait_ge(o_ready, 1)
            sp.dma_start(out[0:(NT - 1) * P, :].rearrange("(t p) f -> p t f", p=P), M["x"][:, 0:NT - 1, :]).then_inc(stored, 16)
            sp.dma_start(out[(NT - 1) * P:N, :], M["x"][0:TAIL, NT - 1, :]).then_inc(stored, 16)
            sp.wait_ge(stored, 32)

        @block.scalar
        def _(act):
            transposed_out(nc, act, M["hT"], [t[:, :].rearrange("p (t c) -> p t c", t=TB) for t in tps], tr_done, tr_copied)
            for t in range(NT):
                act.wait_ge(pr_done, t + 1)
                nc.scalar.activation(haug[:, t, :, 0:F], aps[t % 2][:, 0:H * F].rearrange("p (h f) -> p h f", h=H), ACT.Copy)
                nc.scalar.activation(acol[:, :, t], aps[t % 2][:, H * F:AW], ACT.Copy).then_inc(pr_taken, 1)
            act.wait_ge(at_done, 1)
            nc.scalar.activation(arow_s[:, :], rps[0][0][0:H * NT, 0, 0:P], ACT.Copy).then_inc(at_copied, 1)
            act.sem_inc(ex_done, CREDIT)
            act.wait_ge(wv, 3)

            def window(g, b, nh):
                n = nh * P
                act.wait_ge(rows_mm, g + 1)

                def slope(t):
                    if t >= 2:
                        act.wait_ge(z_done, g * NT + (t - 1))
                    for h in range(H):
                        ins = nc.scalar.activation(t2[:, t % 2, h, 0:n], rps[b][1][:, h, 0:n], ACT.Identity,
                                                   bias=acol5[:, t, h:h + 1])
                    ins.then_inc(t2_done, 1)

                slope(0)
                for t in range(NT):
                    if t + 1 < NT:
                        slope(t + 1)
                    act.wait_ge(z_done, g * NT + (t + 1))
                    act.wait_ge(pm_done, g * NT + max(t + 1, 2))
                    nc.scalar.activation(ex[:, t % 2, :, 0:n], z[:, t % 2, :, 0:n], ACT.Exp).then_inc(ex_done, 1)

            window(0, 0, 2)
            with act.Fori(0, NW // 2 - 1) as i:
                for b in range(2):
                    window(i * 2 + (b + 1), 1 - b, 2)
            window(NW - 2, 1, 2)
            window(NW - 1, 0, 1)
            root_of_variance(nc, act, var_ready, std_ready, M["stats"])
            act.wait_ge(sig, 1)
            nc.scalar.activation(acc_g[:, :, :], M["hT"][:, :, :], ACT.Sigmoid).then_inc(sig, 1)

        @block.vector
        def _(v):
            link = linker(v, dve)
            v.wait_ge(w_in, 48)
            for n in range(2 * H):
                h = n % H
                link(nc.vector.tensor_tensor(scratch, w[:, h * F:(h + 1) * F], att[:, n, :], ALU.mult))
                link(nc.vector.tensor_reduce(w[:, H * F + n:H * F + n + 1], scratch, AX.X, ALU.add))
            nc.vector.memset(haug[:, :, :, F:F + 1], 1.0).then_inc(wv, 1)
            v.wait_ge(wv, 1)
            nc.vector.memset(mx[:, :, :, :], 0.0).then_inc(wv, 1)
            v.wait_ge(pr_taken, NT)
            nc.vector.tensor_scalar(acol5[:, :, :], acol[:, 0:H, :].rearrange("p h t -> p t h"), 0.2, None, ALU.mult).then_inc(wv, 1)
            v.wait_ge(row_in, 16)
            v.sem_inc(group_done, 1)

            group = dict(base=0, step=0)

            def order(ins):
                group["step"] += 1
                ins.then_inc(chain, 1)
                v.wait_ge(chain, group["base"] + group["step"])

            def add_own(g, b, nh):
                v.wait_ge(in_[b], g * (8 * PARTS) + (2 - b) * (8 * PARTS))
                for h in range(nh):
                    own = cnt[b][:, bass.ds(g * 2 + h, 1), h * P:(h + 1) * P]
                    order(nc.vector.tensor_tensor(own, own, M["ident"][:, :].unsqueeze(1), ALU.add))

            def penalties(b, nh, k):
                ts = slice(TB * k, min(TB * k + TB, NT))
                nc.vector.tensor_scalar(pen[:, ts, 0:nh * P], cnt[b][:, ts, 0:nh * P], 0.0, -1e30, ALU.is_equal,
                                        ALU.mult).then_inc(pen_ready, 1)

            def maxima(g, nh, k, h):
                tiles = min(TB, NT - TB * k)
                if h == 0:
                    v.wait_ge(pt_done, g * NTB + (k + 1))
                    v.sem_inc(M["seen"], 1)
                    if k:
                        v.wait_ge(pt_taken, g * NTB + k)
                        v.sem_inc(M["seen"], 1)
                for a in range(H):
                    ins = nc.vector.tensor_tensor_reduce(
                        out=junk[:, h * H + a, 0:tiles * P], in0=tb16[k % 2][:, h, 0:tiles * P],
                        in1=arow[:, a, TB * P * k:TB * P * k + tiles * P], scale=1.0, scalar=-3e38,
                        op0=ALU.add, op1=ALU.max, accum_out=mx[:, h, a, k:k + 1])
                if h == nh - 1:
                    ins.then_inc(pt_taken, 1)

            def exponents(g, nh):
                v.wait_ge(pt_taken, g * NTB + NTB)
                order(nc.vector.tensor_reduce(m[:, 0:nh, :], mx[:, 0:nh, :, :], AX.X, ALU.max))
                adst = acol[:, H:2 * H, bass.ds(g * 2, nh)].rearrange("p a t -> p t a")
                order(nc.vector.tensor_tensor(e[:, 0:nh, :], m[:, 0:nh, :], adst, ALU.add))
                order(nc.vector.scalar_tensor_tensor(m[:, 0:nh, :], e[:, 0:nh, :], 0.2, e[:, 0:nh, :], ALU.mult, ALU.max))
                order(nc.vector.tensor_tensor(r12[:, 0, 0:nh, :], adst, m[:, 0:nh, :], ALU.subtract))
                order(nc.vector.scalar_tensor_tensor(r12[:, 1, 0:nh, :], adst, 0.2, m[:, 0:nh, :], ALU.mult, ALU.subtract))
                for q in range(2):
                    for h in range(nh):
                        for a in range(H):
                            ins = nc.vector.tensor_scalar(diag[:, q, h, a, :], M["ident"][:, :], r12[:, q, h, a:a + 1], None, ALU.mult)
                ins.then_inc(diag_ready, 1)

            def divide(g, nh):
                v.wait_ge(mm_done, g * NT + (NT + CREDIT))
                for h in range(nh):
                    ins = nc.vector.reciprocal(rec[:, h, :], ops[h][:, :, F])
                order(ins)
                for h in range(nh):
                    ins = nc.vector.tensor_scalar(part[:, h, :], ops[h][:, 0, 0:F], rec[:, h, 0:1], None, ALU.mult)
                order(ins)
                for h in range(nh):
                    ins = nc.vector.scalar_tensor_tensor(acc_g[:, bass.ds(g * 2 + h, 1), :], ops[h][:, 1:2, 0:F], rec[:, h, 1:2],
                                                         part[:, h:h + 1, :], ALU.mult, ALU.add)
                ins.then_inc(group_done, 1)

            def window(g, b, nh, ahead, before):
                group["step"] = 0
                n = nh * P
                nb, nn = 1 - b, ahead
                v.wait_ge(rows_mm, g + 1)

                def leaky(t):
                    v.wait_ge(t2_done, g * NT + (t + 1))
                    v.wait_ge(ex_done, g * NT + max(t + 1, 2))
                    for a in range(H):
                        ins = nc.vector.scalar_tensor_tensor(z[:, t % 2, a, 0:n], rps[b][0][:, a, 0:n], acol[:, a, t:t + 1],
                                                             t2[:, t % 2, a, 0:n], ALU.add, ALU.max)
                    ins.then_inc(z_done, 1)

                for t in range(NT):
                    leaky(t)
                    if t == 1 and before:
                        divide(g - 1, 2)
                    if ahead:
                        if t == OWN_AT:
                            add_own(g + 1, nb, nn)
                        if 0 <= t - OWN_AT - 1 < NTB:
                            penalties(nb, nn, t - OWN_AT - 1)
                        k, h = divmod(t - MAX_AT, 2)
                        if 0 <= k < NTB and h < nn:
                            maxima(g + 1, nn, k, h)
                        if t == MAX_AT + 2 * NTB:
                            exponents(g + 1, nn)

            add_own(0, 0, 2)
            for k in range(NTB):
                penalties(0, 2, k)
            for k in range(NTB):
                for h in range(2):
                    maxima(0, 2, k, h)
            exponents(0, 2)
            group["base"] = 7
            window(0, 0, 2, 2, False)
            with v.Fori(0, NW // 2 - 1) as i:
                for b in range(2):
                    group["base"] = i * 18 + (9 * b + 14)
                    window(i * 2 + (b + 1), 1 - b, 2, 2, True)
            group["base"] = 9 * (NW - 2) + 5
            window(NW - 2, 1, 2, 1, True)
            group["base"] = 9 * (NW - 1) + 4
            window(NW - 1, 0, 1, 0, True)
            divide(NW - 1, 1)
            v.wait_ge(group_done, NW + 1)
            full = [P, NT, F]
            g3, h, xc, sq = acc_g[:, :, :], M["h"][:, :, :], M["hT"][:, :, :], haug[:, :, 0, 0:F]
            vec = lambda n: bcast(M["vec"][:, n, :].unsqueeze(1), full)
            link(nc.vector.scalar_tensor_tensor(g3, g3, 0.5, vec(B_GAT), ALU.mult, ALU.add))
            layer_norm(nc, v, link, var_ready, std_ready, h, g3, xc, sq, M["stats"], relu=False)
            link(nc.vector.tensor_tensor(h, h, vec(GAMMA), ALU.mult))
            nc.vector.tensor_tensor(xc, h, vec(BETA), ALU.add).then_inc(sig, 1)
            v.wait_ge(sig, 2)
            link(nc.vector.tensor_tensor(h, xc, g3, ALU.mult))
            nc.vector.tensor_tensor(M["x"][:, :, :], M["x"][:, :, :], h, ALU.add).then_inc(o_ready, 1)

        @block.tensor
        def _(pe):
            transposes(nc, pe, M["h"], M["ident"][:, :], [t[:, :].rearrange("p (t c) -> p t c", t=TB) for t in tps],
                       tr_done, tr_copied)
            pe.wait_ge(tr_copied, NTB)
            pe.wait_ge(wv, 1)
            for t in range(NT):
                if t >= 2:
                    pe.wait_ge(pr_taken, t - 1)
                nc.tensor.matmul(aps[t % 2][:, 0:AW], M["hT"][:, t, :], w[:, :], start=True, stop=True).then_inc(pr_done, 1)
            pe.wait_ge(pr_taken, NT)
            nc.tensor.transpose(rps[0][0][0:H * NT, 0, 0:P], acol[:, 0:H, :].rearrange("p h t -> p (h t)"), M["ident"][:, :]).then_inc(at_done, 1)

            def penalties_out(g, nh, k):
                pe.wait_ge(pen_ready, g * NTB + (k + 1))
                if k >= 2:
                    pe.wait_ge(pt_taken, g * NTB + (k - 1))
                for t in range(TB * k, min(TB * k + TB, NT)):
                    for h in range(nh):
                        ins = nc.tensor.transpose(tb16[k % 2][:, h, (t % TB) * P:(t % TB) * P + P],
                                                  pen[:, t, h * P:(h + 1) * P], M["identb"][:, :])
                ins.then_inc(pt_done, 1)

            def exponent_rows(g, b, nh):
                pe.wait_ge(diag_ready, g + 1)
                for q in range(2):
                    for a in range(H):
                        for h in range(nh):
                            ins = nc.tensor.matmul(rps[b][q][:, a, h * P:(h + 1) * P], M["ones"][:, :], diag[:, q, h, a, :],
                                                   start=True, stop=True)
                ins.then_inc(rows_mm, 1)

            def window(g, b, nh, ahead):
                pe.wait_ge(group_done, g + 1)
                for t in range(NT):
                    pe.wait_ge(pm_done, g * NT + (t + 1 + CREDIT))
                    for h in range(nh):
                        for a in range(H):
                            ins = nc.tensor.matmul(ops[h][:, a, :], pm[:, t % 2, a, h * P:(h + 1) * P], haug[:, t, a, :],
                                                   start=(t == 0 and a == 0), stop=True, skip_group_check=True)
                    ins.then_inc(mm_done, 1)
                    if ahead:
                        k, odd = divmod(t - (MAX_AT - 3), 2)
                        if 2 <= k < NTB and not odd:
                            penalties_out(g + 1, ahead, k)
                        if t in (OWN_AT, OWN_AT + 1):
                            penalties_out(g + 1, ahead, t - OWN_AT)
                        if t == MAX_AT + 2 * NTB:
                            exponent_rows(g + 1, 1 - b, ahead)

            pe.sem_inc(mm_done, CREDIT)
            for k in range(NTB):
                penalties_out(0, 2, k)
            exponent_rows(0, 0, 2)
            window(0, 0, 2, 2)
            with pe.Fori(0, NW // 2 - 1) as i:
                for b in range(2):
                    window(i * 2 + (b + 1), 1 - b, 2, 2)
            window(NW - 2, 1, 2, 1)
            window(NW - 1, 0, 1, 0)

        @block.gpsimd
        def _(pool):
            def window(g, b, nh):
                n = nh * P
                for t in range(NT):
                    pool.wait_ge(ex_done, g * NT + (t + 1 + CREDIT))
                    pool.wait_ge(mm_done, g * NT + max(t + 1, 2))
                    nc.gpsimd.tensor_tensor(pm[:, t % 2, :, 0:n], ex[:, t % 2, :, 0:n],
                                            bcast(cnt[b][:, t:t + 1, 0:n], [P, H, n]), ALU.mult).then_inc(pm_done, 1)

            pool.sem_inc(pm_done, CREDIT)
            with pool.Fori(0, NW // 2) as i:
                for b in range(2):
                    window(i * 2 + b, b, 2)
            window(NW - 1, 0, 1)


NAMES = ['x', 'src', 'dst', 'edge_type_32', 'edge_weight', 'edge_weight1', 'L0_gnn_weight', 'L0_gnn_bias', 'L0_gnn_u',
         'L1_gnn_weight', 'L1_gnn_w_comp', 'L1_gnn_loop_weight', 'L1_gnn_h_bias', 'L2_gnn_W', 'L2_gnn_bias',
         'L2_gnn_prelu_a', 'L3_gnn_gcn_w', 'L3_gnn_gcn_b', 'L3_gnn_gat_w', 'L3_gnn_att_src', 'L3_gnn_att_dst',
         'L3_gnn_gat_b', 'L3_gnn_ln_gamma', 'L3_gnn_ln_beta']


def kernel(**inputs):
    import numpy as _np
    import concourse.bacc as _bacc
    from concourse.bass_utils import run_bass_kernel_spmd as _run

    nc = _bacc.Bacc("TRN2", target_bir_lowering=False, num_devices=1)
    arrays, args = {}, {}
    for name in NAMES:
        a = _np.ascontiguousarray(inputs[name])
        arrays["in_" + name] = a
        args[name] = nc.dram_tensor("in_" + name, a.shape, mybir.dt.from_np(a.dtype), kind="ExternalInput").ap()
    out = nc.dram_tensor("out_0", (N, F), F32, kind="ExternalOutput").ap()
    program(nc, args, out)
    r = _run(nc, [arrays], core_ids=[0])
    return r.results[0]["out_0"]
```
